# Optimizing a Trainium2 kernel written in Bass

```python
import numpy as np
import jax
import jax.numpy as jnp

def _softmax(x, axis=-1):
    return jax.nn.softmax(x, axis=axis)

def _gelu(x):
    return jax.nn.gelu(x, approximate=True)

def _silu(x):
    return jax.nn.silu(x)

def _sigmoid(x):
    return jax.nn.sigmoid(x)

def _layernorm(x, axis=-1, eps=1e-05):
    m = jnp.mean(x, axis=axis, keepdims=True)
    v = jnp.var(x, axis=axis, keepdims=True)
    return (x - m) / jnp.sqrt(v + eps)

def _scatter_add(tgt, idx, src, axis=0):
    return tgt.at[idx].add(src)

def _segment_sum(src, seg, n):
    return jax.ops.segment_sum(src, seg, n)
kernel_name = 'mk_xattn_ffn_d1_seqx_r8_2cee23'

def setup_inputs(seed: int=0):
    np.random.seed(seed)
    _w = jnp.asarray

    def _rec_inputs():
        import jax
        import jax.numpy as jnp
        _rk = jax.random.key(seed)
        x = -0.0002928 + 1 * jax.random.normal(jax.random.fold_in(_rk, 1), (128, 64, 128), jnp.float32)
        _lenS = 64 - jax.random.randint(jax.random.fold_in(_rk, 7), (128,), 0, max(1, 64 // 4) + 1, jnp.int32)
        _lenS2 = 64 - jax.random.randint(jax.random.fold_in(_rk, 8), (128,), 0, max(1, 64 // 4) + 1, jnp.int32)
        _ctx_1024P = jax.random.normal(jax.random.fold_in(_rk, 11), (128, 16, 128), jnp.float32)
        _ctx_1024c = jax.random.dirichlet(jax.random.fold_in(_rk, 511), 0.3 * jnp.ones((16,), jnp.float32), (128, 64))
        _ctx_1024t = jnp.einsum('bsk,bkd->bsd', _ctx_1024c, _ctx_1024P)
        _ctx_1024t = _ctx_1024t * jax.lax.rsqrt(jnp.mean(jnp.square(_ctx_1024t)) + 1e-12) * 0.953939
        ctx_1024 = -1.39393e-06 + 0.999914 * (_ctx_1024t + 0.3 * jax.random.normal(jax.random.fold_in(_rk, 611), (128, 64, 128), jnp.float32))
        _validS = jnp.arange(64)[None, :] < _lenS[:, None]
        _validS2 = jnp.arange(64)[None, :] < _lenS2[:, None]
        _causal = jnp.tril(jnp.ones((64, 64), dtype=bool))
        mask_BxS2_bk0 = jnp.logical_not(jnp.broadcast_to(_validS2[:, :], (128, 64)))
        return (x, ctx_1024, mask_BxS2_bk0)
    x, ctx_1024, mask_BxS2_bk0 = _rec_inputs()

    def _L0_xattn_setup():
        import jax, jax.numpy as jnp
        import numpy as np
        B, L, D, H = (2, 256, 128, 16)
        NEG = 10000000.0

        def pos_encodings(length, d_model, dtype=jnp.float32):
            half = d_model // 2
            periods = 1.0 / 10000.0 ** (jnp.arange(half, dtype=dtype) / half)
            angles = jnp.arange(length, dtype=dtype)[:, None] * periods[None, :]
            return jnp.stack([jnp.sin(angles), jnp.cos(angles)], axis=-1).reshape(length, d_model)
        key = jax.random.key(seed)
        ks = jax.random.split(key, 12)
        scale = 0.02
        q = jax.random.normal(ks[0], (B, L, D), jnp.float32)
        k = jax.random.normal(ks[1], (B, L, D), jnp.float32)
        v = jax.random.normal(ks[2], (B, L, D), jnp.float32)
        mask = jax.random.randint(ks[3], (B, L), 0, 2).astype(bool)
        Wq = jax.random.normal(ks[4], (D, D), jnp.float32) * scale
        Wk = jax.random.normal(ks[5], (D, D), jnp.float32) * scale
        Wv = jax.random.normal(ks[6], (D, D), jnp.float32) * scale
        Wo = jax.random.normal(ks[7], (D, D), jnp.float32) * scale
        bq = jnp.zeros((D,), jnp.float32)
        bk = jnp.zeros((D,), jnp.float32)
        bv = jnp.zeros((D,), jnp.float32)
        bo = jnp.zeros((D,), jnp.float32)
        return {'q': q, 'k': k, 'v': v, 'mask': mask, 'Wq': Wq, 'bq': bq, 'Wk': Wk, 'bk': bk, 'Wv': Wv, 'bv': bv, 'Wo': Wo, 'bo': bo}
    _L0_xattn_all = _L0_xattn_setup()
    _L0_xattn_in = {k: v for k, v in _L0_xattn_all.items() if k in ('Wq', 'bq', 'Wk', 'bk', 'Wv', 'bv', 'Wo', 'bo')}
    del _L0_xattn_all

    def _L0_ffn_setup():
        import jax, jax.numpy as jnp
        import numpy as np
        B, S, D = (2, 128, 128)
        E, H, K, G = (8, 256, 2, 32)
        key = jax.random.key(seed)
        ks = jax.random.split(key, 5)
        return {'x': jax.random.normal(ks[0], (B, S, D), jnp.float32), 'wg1': jax.random.normal(ks[1], (D, G), jnp.float32) * 0.02, 'bg1': jnp.zeros((G,), jnp.float32), 'wg2': jax.random.normal(ks[2], (G, E), jnp.float32) * 0.02, 'w_in': jax.random.uniform(ks[3], (E, D, H), jnp.float32, -1.0 / D, 1.0 / D), 'w_out': jax.random.uniform(ks[4], (E, H, D), jnp.float32, -1.0 / H, 1.0 / H)}
    _L0_ffn_all = _L0_ffn_setup()
    _L0_ffn_in = {k: v for k, v in _L0_ffn_all.items() if k in ('wg1', 'bg1', 'wg2', 'w_in', 'w_out')}
    del _L0_ffn_all
    return {'x': x, 'ctx_1024': ctx_1024, 'mask_BxS2_bk0': mask_BxS2_bk0, 'L0_xattn_Wq': _L0_xattn_in['Wq'], 'L0_xattn_bq': _L0_xattn_in['bq'], 'L0_xattn_Wk': _L0_xattn_in['Wk'], 'L0_xattn_bk': _L0_xattn_in['bk'], 'L0_xattn_Wv': _L0_xattn_in['Wv'], 'L0_xattn_bv': _L0_xattn_in['bv'], 'L0_xattn_Wo': _L0_xattn_in['Wo'], 'L0_xattn_bo': _L0_xattn_in['bo'], 'L0_ffn_wg1': _L0_ffn_in['wg1'], 'L0_ffn_bg1': _L0_ffn_in['bg1'], 'L0_ffn_wg2': _L0_ffn_in['wg2'], 'L0_ffn_w_in': _L0_ffn_in['w_in'], 'L0_ffn_w_out': _L0_ffn_in['w_out']}

def reference(x, ctx_1024, mask_BxS2_bk0, L0_xattn_Wq, L0_xattn_bq, L0_xattn_Wk, L0_xattn_bk, L0_xattn_Wv, L0_xattn_bv, L0_xattn_Wo, L0_xattn_bo, L0_ffn_wg1, L0_ffn_bg1, L0_ffn_wg2, L0_ffn_w_in, L0_ffn_w_out):
    import jax
    import jax.numpy as jnp

    def _L0_xattn_ref(q, k, v, mask, Wq, bq, Wk, bk, Wv, bv, Wo, bo):
        import jax, jax.numpy as jnp
        import numpy as np
        B, L, D, H = (2, 256, 128, 16)
        NEG = 10000000.0

        def pos_encodings(length, d_model, dtype=jnp.float32):
            half = d_model // 2
            periods = 1.0 / 10000.0 ** (jnp.arange(half, dtype=dtype) / half)
            angles = jnp.arange(length, dtype=dtype)[:, None] * periods[None, :]
            return jnp.stack([jnp.sin(angles), jnp.cos(angles)], axis=-1).reshape(length, d_model)
        b, l, d_model = q.shape
        d_head = d_model // H
        pe = pos_encodings(l, d_model, q.dtype)
        qp = (q + pe) @ Wq.T + bq
        kp = (k + pe) @ Wk.T + bk
        vp = v @ Wv.T + bv

        def split_heads(x):
            return x.reshape(b, l, H, d_head).transpose(0, 2, 1, 3)
        qh, kh, vh = (split_heads(qp), split_heads(kp), split_heads(vp))
        scores = jnp.einsum('bhqd,bhkd->bhqk', qh, kh) * d_head ** (-0.5)
        causal = jnp.triu(jnp.ones((l, l), bool), k=1)
        m = mask[:, None, None, :] | causal[None, None, :, :]
        scores = scores - m.astype(scores.dtype) * NEG
        attn = jax.nn.softmax(scores, axis=-1)
        out = jnp.einsum('bhqk,bhkd->bhqd', attn, vh)
        out = out.transpose(0, 2, 1, 3).reshape(b, l, d_model)
        return out @ Wo.T + bo

    def _L0_ffn_ref(x, wg1, bg1, wg2, w_in, w_out):
        import jax, jax.numpy as jnp
        import numpy as np
        B, S, D = (2, 128, 128)
        E, H, K, G = (8, 256, 2, 32)
        b, s, d = x.shape
        xt = x.reshape(-1, d)
        n = xt.shape[0]
        g = jax.nn.gelu(xt @ wg1 + bg1, approximate=False)
        logits = g @ wg2
        probs = jax.nn.softmax(logits, axis=-1)
        top_vals, top_idx = jax.lax.top_k(probs, K)
        gates = jnp.zeros_like(probs).at[jnp.arange(n)[:, None], top_idx].set(top_vals)
        h = jax.nn.gelu(jnp.einsum('nd,edh->enh', xt, w_in), approximate=False)
        o = jnp.einsum('enh,ehd->end', h, w_out)
        y = jnp.einsum('ne,end->nd', gates, o)
        return y.reshape(b, s, d)
    x = x + _L0_xattn_ref(_layernorm(x, axis=-1), ctx_1024, ctx_1024, mask_BxS2_bk0, L0_xattn_Wq, L0_xattn_bq, L0_xattn_Wk, L0_xattn_bk, L0_xattn_Wv, L0_xattn_bv, L0_xattn_Wo, L0_xattn_bo)
    x = x + _L0_ffn_ref(_layernorm(x, axis=-1), L0_ffn_wg1, L0_ffn_bg1, L0_ffn_wg2, L0_ffn_w_in, L0_ffn_w_out)
    return x

_drawn_inputs = setup_inputs


def setup_inputs(seed=0):
    import zlib

    import numpy as np

    out = dict(_drawn_inputs(seed))
    spreads = {'L0_xattn_bq': (0.0, 2.0),
     'L0_xattn_bk': (0.0, 2.0),
     'L0_xattn_bv': (0.0, 0.343),
     'L0_xattn_bo': (0.0, 0.1),
     'L0_ffn_bg1': (0.0, 2.0)}
    factors = {'L0_xattn_Wq': 8.0,
     'L0_xattn_Wk': 8.0,
     'L0_ffn_wg1': 8.0,
     'L0_ffn_wg2': 8.0,
     'L0_ffn_w_in': 8.0,
     'L0_ffn_w_out': 8.0}
    for name, (base, spread) in spreads.items():
        noise = np.random.default_rng([zlib.crc32(name.encode()), seed]).standard_normal(out[name].shape)
        drawn = base * np.exp(spread * noise) if base else spread * noise
        out[name] = jnp.asarray(drawn.astype(out[name].dtype))
    for name, factor in factors.items():
        out[name] = (out[name] * factor).astype(out[name].dtype)
    return out
```

```python
from contextlib import ExitStack

import numpy as np

import concourse.bass as bass
from concourse import mybir

F32 = mybir.dt.float32
U8 = mybir.dt.uint8
ALU = mybir.AluOpType
ACT = mybir.ActivationFunctionType
AX = mybir.AxisListType.X

P = 128
B, L, D = 128, 64, 128
H = 16
DH = D // H
HH = H // 2
E, HID, G = 8, 256, 32
N = B * L
NT = N // P
U = 4
NS = NT // U
SCALE = float(DH) ** -0.5
NEG = 10000000.0
EPS = 1e-5
VM = 64
J = H // 2


def position_encodings():
    half = D // 2
    periods = np.float32(1.0) / np.float32(10000.0) ** (np.arange(half, dtype=np.float32) / np.float32(half))
    angles = np.arange(L, dtype=np.float32)[:, None] * periods[None, :].astype(np.float32)
    return np.stack([np.sin(angles), np.cos(angles)], axis=-1).reshape(L, D).astype(np.float32)


def build(nc, x, ctxT, mask, wqT, bq, wkT, bk, wvT, bv, woT, bo, wg1, bg1, wg2, w_in, w_out, out):
    pe_c = nc.inline_tensor(np.ascontiguousarray(position_encodings().T), name="pe_t")
    ident_c = nc.inline_tensor(np.eye(P, dtype=np.float32), name="ident")
    head_of_row = (np.arange(P) % (D // 2)) // DH
    headmask_c = nc.inline_tensor((head_of_row[:, None] == np.arange(HH)[None, :]).astype(np.float32), name="headmask")
    q_of_row = np.arange(P) % L
    causal_c = nc.inline_tensor(
        np.where(np.arange(L)[None, :] > q_of_row[:, None], -NEG, 0.0).astype(np.float32), name="causal")
    ones_cols = np.zeros((P, VM), np.float32)
    for p in range(2):
        ones_cols[p * L:(p + 1) * L, 4 * DH + p] = 1.0
    ones_c = nc.inline_tensor(ones_cols, name="value_ones")
    iota_c = nc.inline_tensor(np.tile(np.arange(E, dtype=np.float32) - E, (P, 1)), name="iota_e")

    x1_d = nc.dram_tensor("x1_scratch", [N, D], F32, kind="Internal").ap()
    xt2_d = nc.dram_tensor("xt2_scratch", [D, N], F32, kind="Internal").ap()

    x_r = x.rearrange("(t p) d -> p t d", p=P)
    out_r = out.rearrange("(t p) d -> p t d", p=P)
    x1_r = x1_d.rearrange("(t p) d -> p t d", p=P)

    with ExitStack() as ctx:
        def sb(name, shape, dt=F32):
            return ctx.enter_context(nc.sbuf_tensor(name, shape, dt))

        def sem(name):
            return ctx.enter_context(nc.semaphore(name))

        bank = [ctx.enter_context(nc.psum_tensor(f"bank{i}", [P, 512], F32)) for i in range(8)]
        W0, W1, SA, SB, PTA, PTB, XB, YB = bank
        S_bank, PT_bank = [SA, SB], [PTA, PTB]

        wq_s, wk_s, wv_s, wo_s = (sb(n, [P, D]) for n in ("wq_s", "wk_s", "wv_s", "wo_s"))
        bq_s, bk_s = sb("bq_s", [P, 1]), sb("bk_s", [P, 1])
        bv_s, bo_s = sb("bv_s", [P, 1]), sb("bo_s", [P, D])
        bvb_s, cvec = sb("bvb_s", [P, P]), sb("cvec", [P, D])
        pe_s, ident = sb("pe_s", [P, L]), sb("ident_s", [P, P])
        headmask, causal = sb("headmask_s", [P, HH]), sb("causal_s", [P, L])
        iota_e = sb("iota_e_s", [P, E])
        ones_s = sb("ones_s", [P, VM])
        wg1_s, bg1_s, wg2_s = sb("wg1_s", [D, G]), sb("bg1_s", [G, 1]), sb("wg2_s", [G, E])
        win_s = sb("win_s", [P, E, HID])
        wout_s = sb("wout_s", [P, E, 2, D])

        x_in = sb("x_in", [P, U, D])
        ctx_k = sb("ctx_k", [P, U * P])
        ctx_v = sb("ctx_v", [P, U * P])
        mask_in = sb("mask_in", [P, U, L], U8)
        negmask = sb("negmask", [P, U, L])
        x_res = sb("x_res", [P, U, D])
        stat1, mv1, rstd1 = sb("stat1", [P, U, 6]), sb("mv1", [P, U, 2]), sb("rstd1", [P, U])
        xn = sb("xn", [P, U, D])
        minus_half, eps_s = sb("minus_half", [P, U]), sb("eps_s", [P, U])
        var1 = sb("var1", [P, U])
        xT = sb("xT", [P, U * P])
        q2 = sb("q2", [P, 2, U, P])
        k2 = sb("k2", [P, 2, U, L])
        kx = sb("kx", [P, U, 2, HH, L])
        vx = sb("vx", [P, U, J, VM])
        sm = sb("sm", [P, 2, H, L])
        smax = sb("smax", [P, H])
        pt = sb("pt", [P, J, P])
        xo = sb("xo", [P, 4, P])
        rden = sb("rden", [P, J, 2])
        on = sb("on", [P, D])
        onT = sb("onT", [P, P])
        x1 = sb("x1", [P, U, D])

        logits = sb("logits", [P, NT, E])
        probs = sb("probs", [P, NT, E])
        gates = sb("gates", [P, NT, E])
        t_a, t_b = sb("t_a", [P, NT, E]), sb("t_b", [P, NT, E])
        r_a, r_b = sb("r_a", [P, NT]), sb("r_b", [P, NT])

        xt2 = sb("xt2", [P, U * P])
        g_s = sb("g_s", [G, U * P])
        xt2_f = sb("xt2_f", [P, 2, U * P])
        acc = sb("acc", [P, 2, U, D])
        gcur = sb("gcur", [P, 2, U, E])
        h_s = sb("h_s", [P, 4, U * P])
        (s_rt, s_rte, s_rst, s_rg, s_rge, s_rl, s_log, s_ch, s_up, s_gl, s_dn, s_ac,
         s_gc, s_rex) = (sem(n) for n in (
             "xn2_transposed", "xt2_ready", "xt2_stored", "hidden_in_psum", "hidden_ready",
             "logits_in_psum", "logits_ready", "chain", "up_in_psum",
             "gelu_ready", "down_in_psum", "acc_ready", "gates_picked", "route_exp"))
        s_fx, s_fa, s_out = [[sem(f"{n}{i}") for i in range(2)] for n in ("ffn_x_loaded", "ffn_acc_loaded", "stored")]

        s_w, s_x, s_ck, s_cv, s_m = (sem(n) for n in ("weights_in", "x_loaded", "ctx_k_loaded", "ctx_v_loaded", "mask_loaded"))
        s_xr = [sem(f"x_res_loaded{u}") for u in range(U)]
        s_x1st = [sem(f"x1_stored{u}") for u in range(U)]
        (s_zero, s_stat, s_xn, s_cp, s_neg, s_xt, s_xTs, s_k, s_kev, s_q, s_qev, s_v, s_vev, s_kx,
         s_sc, s_stt, s_max, s_sub, s_exp, s_pt, s_ptev, s_pv, s_xev, s_tq, s_rden, s_norm, s_ont,
         s_ontev, s_y, s_xres, s_res, s_bvb, s_cv, s_cvec, s_r1, s_st1, s_cv_ps, s_va1, s_mh) = (sem(n) for n in (
             "zeroed", "ln1_stats", "xn_ready", "ctx_k_ready", "negmask_ready", "xT_in_psum", "xT_ready",
             "k_in_psum", "k2_ready", "q_in_psum", "q2_ready", "v_in_psum", "vx_ready", "kx_ready",
             "scores_in_psum", "scores_masked", "row_max", "scores_shifted", "probs_ready", "pt_in_psum",
             "pt_ready", "pv_in_psum", "xo_ready", "o_in_psum", "rden_ready", "o_normed", "onT_in_psum",
             "onT_ready", "y_in_psum", "x_res_ready", "x1_ready",
             "bv_spread", "cvec_in_psum", "cvec_ready", "ln1_rstd", "ln1_bn", "bias_in_psum",
             "ln1_var_eps", "minus_half_set"))
        NW = 19

        with nc.Block() as block:

            @block.sync
            def _(sp):
                for dst, src in ((wq_s[:, :], wqT), (wk_s[:, :], wkT), (wv_s[:, :], wvT), (wo_s[:, :], woT),
                                 (bq_s[:, :], bq.rearrange("(p a) -> p a", a=1)),
                                 (bk_s[:, :], bk.rearrange("(p a) -> p a", a=1)),
                                 (bv_s[:, :], bv.rearrange("(p a) -> p a", a=1)),
                                 (bo_s[:, :], bo.partition_broadcast(P)),
                                 (pe_s[:, :], pe_c.ap()), (ident[:, :], ident_c.ap()),
                                 (headmask[:, :], headmask_c.ap()), (causal[:, :], causal_c.ap()),
                                 (iota_e[:, :], iota_c.ap()), (ones_s[:, :], ones_c.ap()),
                                 (wg1_s[:, :], wg1), (bg1_s[:, :], bg1.rearrange("(p a) -> p a", a=1)),
                                 (wg2_s[:, :], wg2),
                                 (win_s[:, :, :], w_in.rearrange("e d h -> d e h")),
                                 (wout_s[:, :, :, :].rearrange("p e c d -> p (e c) d"),
                                  w_out.rearrange("e (c p) d -> p (e c) d", p=P))):
                    sp.dma_start(dst, src).then_inc(s_w, 16)

                def load_x(s):
                    sp.dma_start(x_in[:, :, :], x_r[:, bass.ds(s * U, U), :]).then_inc(s_x, 16)

                def load_ctx_k(s):
                    sp.dma_start(ctx_k[:, :], ctxT[:, bass.ds(s * (U * P), U * P)]).then_inc(s_ck, 16)

                def load_ctx_v(s):
                    sp.dma_start(ctx_v[:, :], ctxT[:, bass.ds(s * (U * P), U * P)]).then_inc(s_cv, 16)

                def load_mask(s):
                    for b in range(2):
                        src = mask[bass.ds(s * (2 * U), 2 * U), :].rearrange("(u b) k -> b u k", b=2)[b]
                        sp.dma_start(mask_in[b * L:(b + 1) * L, :, :], src.partition_broadcast(L)).then_inc(s_m, 16)

                def load_x_res(s, u):
                    sp.dma_start(x_res[:, u, :], x_r[:, bass.ds(s * U + u, 1), :].rearrange("p a d -> p (a d)")
                                 ).then_inc(s_xr[u], 16)

                def store_tile(s, u):
                    t = s * U + u
                    sp.wait_ge(s_res, t + 1)
                    sp.dma_start(x1_r[:, bass.ds(t, 1), :].rearrange("p a d -> p (a d)"), x1[:, u, :]
                                 ).then_inc(s_x1st[u], 16)

                load_x(0)
                load_ctx_k(0)
                load_ctx_v(0)
                load_mask(0)
                for u in range(U):
                    load_x_res(0, u)
                sp.wait_ge(s_xn, 1)
                load_x(1)
                sp.wait_ge(s_k, 1)
                load_ctx_k(1)
                sp.wait_ge(s_v, 1)
                load_ctx_v(1)
                sp.wait_ge(s_neg, 1)
                load_mask(1)

                def body(s, first, before_last, last):
                    for u in range(U):
                        if not (first and u == 0):
                            ps, pu = (s, u - 1) if u else (s - 1, U - 1)
                            store_tile(ps, pu)
                            if not (last and u):
                                load_x_res(ps + 1, pu)
                        if before_last or last:
                            continue
                        if u == 0:
                            sp.wait_ge(s_xn, s + 2)
                            load_x(s + 2)
                        if u == 1:
                            sp.wait_ge(s_k, s + 2)
                            load_ctx_k(s + 2)
                        if u == 2:
                            sp.wait_ge(s_neg, s + 2)
                            load_mask(s + 2)
                        if u == 3:
                            sp.wait_ge(s_v, s + 2)
                            load_ctx_v(s + 2)

                body(0, True, False, False)
                with sp.Fori(1, NS - 2) as s:
                    body(s, False, False, False)
                body(NS - 2, False, True, False)
                body(NS - 1, False, False, True)
                store_tile(NS - 1, U - 1)
                for u in range(U):
                    sp.wait_ge(s_x1st[u], 16 * NS)

            @block.tensor
            def _(pe):
                def t_x(s):
                    pe.wait_ge(s_xn, s + 1)
                    for u in range(U):
                        last = nc.tensor.transpose(W0[:, u * P:(u + 1) * P], xn[:, u, :], ident[:, :])
                    last.then_inc(s_xt, 1)

                def project_k(s):
                    pe.wait_ge(s_cp, s + 1)
                    nc.tensor.matmul(W1[:, :], wk_s[:, :], ctx_k[:, :], start=True, stop=True).then_inc(s_k, 1)

                def project_q(s):
                    pe.wait_ge(s_xTs, s + 1)
                    nc.tensor.matmul(W0[:, :], wq_s[:, :], xT[:, :], start=True, stop=True).then_inc(s_q, 1)

                def project_v(s):
                    pe.wait_ge(s_cv, 16 * (s + 1))
                    pe.wait_ge(s_qev, s + 1)
                    for u in range(U):
                        last = nc.tensor.matmul(W0[:, u * P:(u + 1) * P], ctx_v[:, u * P:(u + 1) * P], wv_s[:, :],
                                                start=True, stop=True)
                    last.then_inc(s_v, 1)

                def scores(t, u):
                    pe.wait_ge(s_kx, t + 1)
                    for half in range(2):
                        nc.tensor.matmul(S_bank[half][:, :], q2[:, half, u, :],
                                         kx[:, u, half, :, :].rearrange("p h k -> p (h k)"),
                                         start=True, stop=True).then_inc(s_sc, 1)

                def transpose_probs(t, u):
                    pe.wait_ge(s_exp, t + 1)
                    pr = sm[:, u % 2, :, :].rearrange("p h k -> p (h k)")
                    for j in range(J):
                        last = nc.tensor.transpose(PT_bank[j // 4][:, (j % 4) * P:(j % 4 + 1) * P],
                                                   pr[:, j * P:(j + 1) * P], ident[:, :])
                        if j % 4 == 3:
                            last.then_inc(s_pt, 1)

                def values(t, u):
                    pe.wait_ge(s_ptev, 2 * t + 2)
                    for j in range(J):
                        o = VM * (j % 2)
                        last = nc.tensor.matmul(XB[o:o + VM, (j // 2) * P:(j // 2 + 1) * P], vx[:, u, j, :],
                                                pt[:, j, :], start=True, stop=True)
                    last.then_inc(s_pv, 1)

                def queries_to_rows(t):
                    pe.wait_ge(s_xev, t + 1)
                    for c in range(4):
                        last = nc.tensor.transpose(YB[:, c * P:(c + 1) * P], xo[:, c, :], ident[:, :])
                    last.then_inc(s_tq, 1)

                def transpose_o(t):
                    pe.wait_ge(s_norm, t + 1)
                    nc.tensor.transpose(YB[:, 0:P], on[:, :], ident[:, :]).then_inc(s_ont, 1)

                def project_o(t):
                    pe.wait_ge(s_ontev, t + 1)
                    nc.tensor.matmul(YB[:, P:2 * P], onT[:, :], wo_s[:, :], start=True, stop=True).then_inc(s_y, 1)

                pe.wait_ge(s_w, 16 * NW)
                pe.wait_ge(s_bvb, 1)
                nc.tensor.matmul(YB[:, 0:D], bvb_s[:, :], wo_s[:, :], start=True, stop=True).then_inc(s_cv_ps, 1)
                t_x(0)
                project_k(0)
                project_q(0)
                project_v(0)
                pe.wait_ge(s_zero, 2)
                pe.wait_ge(s_qev, 1)
                scores(0, 0)
                pe.wait_ge(s_cvec, 1)

                def body(s, first, last):
                    for u in range(U):
                        t = s * U + u
                        before = not (first and u == 0)
                        after = not (last and u == U - 1)
                        if after:
                            pe.wait_ge(s_stt, 2 * t + 2)
                            if u == U - 1:
                                pe.wait_ge(s_qev, s + 2)
                            scores(t + 1, (u + 1) % U)
                        if before:
                            if not (first and u == 1):
                                pe.wait_ge(s_res, t - 1)
                            queries_to_rows(t - 1)
                        transpose_probs(t, u)
                        if before:
                            transpose_o(t - 1)
                        if not last:
                            if u == 0:
                                pe.wait_ge(s_vev, s + 1)
                                t_x(s + 1)
                            if u == 1:
                                pe.wait_ge(s_kev, s + 1)
                                project_k(s + 1)
                            if u == 2:
                                project_q(s + 1)
                            if u == 3:
                                project_v(s + 1)
                        if before:
                            project_o(t - 1)
                        if u == 0:
                            pe.wait_ge(s_vev, s + 1)
                        values(t, u)

                body(0, True, False)
                with pe.Fori(1, NS - 1) as s:
                    body(s, False, False)
                body(NS - 1, False, True)
                pe.wait_ge(s_res, NT - 1)
                queries_to_rows(NT - 1)
                transpose_o(NT - 1)
                project_o(NT - 1)

            @block.scalar
            def _(act):
                def k_evac(s):
                    act.wait_ge(s_k, s + 1)
                    src = W1[:, :].rearrange("c (u b k) -> c u b k", u=U, b=2)
                    for half in range(2):
                        r = slice(half * 64, half * 64 + 64)
                        for b in range(2):
                            last = nc.scalar.activation(k2[b * 64:b * 64 + 64, half, :, :], src[r, :, b, :],
                                                        ACT.Identity, bias=bk_s[r, :])
                    last.then_inc(s_kev, 1)

                def q_evac(s):
                    act.wait_ge(s_q, s + 1)
                    src = W0[:, :].rearrange("c (u b k) -> c u b k", u=U, b=2)
                    for half in range(2):
                        r = slice(half * 64, half * 64 + 64)
                        for b in range(2):
                            last = nc.scalar.activation(q2[b * 64:b * 64 + 64, half, :, b * L:(b + 1) * L],
                                                        src[r, :, b, :], ACT.Identity, bias=bq_s[r, :])
                    last.then_inc(s_qev, 1)

                def v_evac(s):
                    act.wait_ge(s_v, s + 1)
                    src = W0[:, :].rearrange("r (uj p c) -> r uj p c", p=2, c=DH)
                    dst = vx[:, :, :, :].rearrange("r u j m -> r (u j) m")
                    for b in range(2):
                        for p in range(2):
                            o = (2 * b + p) * DH
                            last = nc.scalar.activation(dst[p * 64:p * 64 + 64, :, o:o + DH],
                                                        src[b * 64:b * 64 + 64, :, p, :], ACT.Copy)
                    last.then_inc(s_vev, 1)

                def exps(t, u):
                    act.wait_ge(s_sub, t + 1)
                    nc.scalar.activation(sm[:, u % 2, :, :], sm[:, u % 2, :, :], ACT.Exp).then_inc(s_exp, 1)

                def onT_evac(t):
                    act.wait_ge(s_ont, t + 1)
                    nc.scalar.activation(onT[:, :], YB[:, 0:P], ACT.Copy).then_inc(s_ontev, 1)

                act.wait_ge(s_w, 16 * NW)
                act.wait_ge(s_zero, 2)
                k_evac(0)
                q_evac(0)
                v_evac(0)
                exps(0, 0)

                def body(s, first, last):
                    for u in range(U):
                        t = s * U + u
                        for i in range(2):
                            act.wait_ge(s_pt, 2 * t + i + 1)
                            nc.scalar.activation(pt[:, 4 * i:4 * i + 4, :].rearrange("p j q -> p (j q)"),
                                                 PT_bank[i][:, :], ACT.Copy).then_inc(s_ptev, 1)
                        if not (first and u == 0):
                            onT_evac(t - 1)
                        if not last:
                            if u == 1:
                                act.wait_ge(s_kx, t + 3)
                                k_evac(s + 1)
                            if u == 2:
                                q_evac(s + 1)
                        act.wait_ge(s_pv, t + 1)
                        nc.scalar.activation(xo[:, :, :].rearrange("p c q -> p (c q)"), XB[:, :], ACT.Copy
                                             ).then_inc(s_xev, 1)
                        if not last and u == 3:
                            v_evac(s + 1)
                        if not (last and u == U - 1):
                            exps(t + 1, u + 1)

                body(0, True, False)
                with act.Fori(1, NS - 1) as s:
                    body(s, False, False)
                body(NS - 1, False, True)
                onT_evac(NT - 1)

            @block.vector
            def _(dve):
                def ln1_stats(s):
                    dve.wait_ge(s_x, 16 * (s + 1))
                    for u in range(U):
                        last = nc.vector.bn_stats(stat1[:, u, :], x_in[:, u, :])
                    last.then_inc(s_st1, 1)

                def ln1_variance():
                    for u in range(U):
                        last = nc.vector.bn_aggr(mv1[:, u, :], stat1[:, u, :])
                    last.then_inc(s_stat, 1)

                def ln1_norm(s):
                    dve.wait_ge(s_r1, s + 1)
                    for u in range(U):
                        last = nc.vector.tensor_scalar(xn[:, u, :], x_in[:, u, :], mv1[:, u, 0:1],
                                                       rstd1[:, u:u + 1], ALU.subtract, ALU.mult)
                    last.then_inc(s_xn, 1)

                def x_evac(s):
                    dve.wait_ge(s_xt, s + 1)
                    nc.vector.tensor_tensor(xT[:, :].rearrange("p (b k) -> p b k", k=L),
                                            W0[:, :].rearrange("p (b k) -> p b k", k=L),
                                            pe_s[:, :].unsqueeze(1).broadcast_to([P, 2 * U, L]), ALU.add
                                            ).then_inc(s_xTs, 1)

                def make_mask(s):
                    dve.wait_ge(s_m, 32 * (s + 1))
                    nc.vector.scalar_tensor_tensor(out=negmask[:, :, :], in0=mask_in[:, :, :], scalar=-NEG,
                                                   in1=causal[:, :].unsqueeze(1).broadcast_to([P, U, L]),
                                                   op0=ALU.mult, op1=ALU.min).then_inc(s_neg, 1)

                def mask_scores(t, u):
                    for half in range(2):
                        dve.wait_ge(s_sc, 2 * t + half + 1)
                        nc.vector.scalar_tensor_tensor(
                            out=sm[:, u % 2, half * HH:(half + 1) * HH, :],
                            in0=S_bank[half][:, :].rearrange("p (h k) -> p h k", k=L), scalar=SCALE,
                            in1=negmask[:, u, :].unsqueeze(1).broadcast_to([P, HH, L]),
                            op0=ALU.mult, op1=ALU.add).then_inc(s_stt, 1)

                def shift_scores(t, u):
                    dve.wait_ge(s_stt, 2 * t + 2)
                    nc.vector.reduce_max(smax[:, :], sm[:, u % 2, :, :], AX).then_inc(s_max, 1)
                    dve.wait_ge(s_max, t + 1)
                    nc.vector.tensor_tensor(sm[:, u % 2, :, :], sm[:, u % 2, :, :],
                                            smax[:, :].unsqueeze(2).broadcast_to([P, H, L]),
                                            ALU.subtract).then_inc(s_sub, 1)

                def normalise(t):
                    dve.wait_ge(s_tq, t + 1)
                    y = YB[:, :].rearrange("r (j m) -> r j m", m=VM)
                    nc.vector.reciprocal(rden[:, :, :], y[:, :, 4 * DH:4 * DH + 2]).then_inc(s_rden, 1)
                    dve.wait_ge(s_rden, t + 1)
                    for b in range(2):
                        r = slice(b * 64, b * 64 + 64)
                        last = nc.vector.tensor_tensor(
                            on[r, :].rearrange("r (j p c) -> r j p c", p=2, c=DH),
                            y[r, :, 2 * DH * b:2 * DH * (b + 1)].rearrange("r j (p c) -> r j p c", p=2),
                            rden[r, :, :].unsqueeze(3).broadcast_to([64, J, 2, DH]), ALU.mult)
                    last.then_inc(s_norm, 1)

                def residual(t, u, reused):
                    dve.wait_ge(s_y, t + 1)
                    dve.wait_ge(s_xres, t + 1)
                    if reused is not None:
                        dve.wait_ge(s_x1st[u], reused)
                    nc.vector.tensor_tensor(x1[:, u, :], YB[:, P:2 * P], x_res[:, u, :], ALU.add).then_inc(s_res, 1)

                nc.vector.memset(q2[:, :, :, :], 0.0).then_inc(s_zero, 1)
                dve.wait_ge(s_w, 16 * NW)
                for u in range(U):
                    last = nc.vector.tensor_copy(vx[:, u, :, :], ones_s[:, :].unsqueeze(1).broadcast_to([P, J, VM]))
                last.then_inc(s_zero, 1)
                nc.vector.tensor_copy(bvb_s[:, :], bv_s[:, 0:1].broadcast_to([P, P])).then_inc(s_bvb, 1)
                dve.wait_ge(s_cv_ps, 1)
                nc.vector.tensor_tensor(cvec[:, :], YB[:, 0:D], bo_s[:, :], ALU.add).then_inc(s_cvec, 1)
                ln1_stats(0)
                dve.wait_ge(s_st1, 1)
                ln1_variance()
                make_mask(0)
                ln1_norm(0)
                x_evac(0)
                ln1_stats(1)
                dve.wait_ge(s_st1, 2)
                ln1_variance()
                dve.wait_ge(s_xt, 1)
                ln1_norm(1)
                dve.wait_ge(s_neg, 1)
                mask_scores(0, 0)
                shift_scores(0, 0)

                def body(s, first, second, before_last, last):
                    for u in range(U):
                        t = s * U + u
                        before = not (first and u == 0)
                        after = not (last and u == U - 1)
                        if after:
                            if not first or u > 0:
                                dve.wait_ge(s_pt, 2 * t)
                            if u == U - 1:
                                dve.wait_ge(s_neg, s + 2)
                            if u == 2 and not (last or before_last):
                                dve.wait_ge(s_st1, s + 3)
                            mask_scores(t + 1, (u + 1) % U)
                            if u == 2 and not (last or before_last):
                                ln1_variance()
                        if before:
                            normalise(t - 1)
                        if after:
                            shift_scores(t + 1, (u + 1) % U)
                        if before:
                            reused = None if first or (second and not u) else 16 * (s if u else s - 1)
                            residual(t - 1, (u - 1) % U, reused)
                        if not last:
                            if u == 0:
                                x_evac(s + 1)
                            if u == 2:
                                make_mask(s + 1)
                        if not (last or before_last):
                            if u == 1:
                                ln1_stats(s + 2)
                            if u == 3:
                                dve.wait_ge(s_xt, s + 2)
                                ln1_norm(s + 2)

                body(0, True, False, False, False)
                body(1, False, True, False, False)
                with dve.Fori(2, NS - 2) as s:
                    body(s, False, False, False, False)
                body(NS - 2, False, False, True, False)
                body(NS - 1, False, False, False, True)
                normalise(NT - 1)
                residual(NT - 1, U - 1, 16 * (NS - 1))

            @block.gpsimd
            def _(pool):
                def add_positions(s):
                    pool.wait_ge(s_ck, 16 * (s + 1))
                    v = ctx_k[:, :].rearrange("p (b k) -> p b k", k=L)
                    nc.gpsimd.tensor_tensor(v, v, pe_s[:, :].unsqueeze(1).broadcast_to([P, 2 * U, L]),
                                            ALU.add).then_inc(s_cp, 1)

                def rstd_1(s):
                    pool.wait_ge(s_stat, s + 1)
                    nc.gpsimd.tensor_tensor(var1[:, :], mv1[:, :, 1], eps_s[:, :], ALU.add).then_inc(s_va1, 1)
                    pool.wait_ge(s_va1, s + 1)
                    nc.gpsimd.tensor_tensor(rstd1[:, :], var1[:, :], minus_half[:, :], ALU.pow).then_inc(s_r1, 1)

                def spread_keys(t, u, reused=True):
                    if reused:
                        pool.wait_ge(s_sc, 2 * (t - 4) + 2)
                    for half in range(2):
                        last = nc.gpsimd.tensor_tensor(
                            kx[:, u, half, :, :], k2[:, half, u, :].unsqueeze(1).broadcast_to([P, HH, L]),
                            headmask[:, :].unsqueeze(2).broadcast_to([P, HH, L]), ALU.mult)
                    last.then_inc(s_kx, 1)

                def residual_bias(s, u):
                    pool.wait_ge(s_xr[u], 16 * (s + 1))
                    nc.gpsimd.tensor_tensor(x_res[:, u, :], x_res[:, u, :], cvec[:, :], ALU.add).then_inc(s_xres, 1)

                nc.gpsimd.memset(minus_half[:, :], -0.5).then_inc(s_mh, 1)
                nc.gpsimd.memset(eps_s[:, :], EPS).then_inc(s_mh, 1)
                pool.wait_ge(s_mh, 2)
                pool.wait_ge(s_w, 16 * NW)
                add_positions(0)
                rstd_1(0)
                pool.wait_ge(s_kev, 1)
                spread_keys(0, 0, False)
                rstd_1(1)
                for u in range(1, U):
                    spread_keys(u, u, False)
                pool.wait_ge(s_cvec, 1)

                def body(s, before_last, last):
                    for u in range(U):
                        if u == 0 and not last:
                            add_positions(s + 1)
                        residual_bias(s, u)
                        if not last:
                            if u == 2:
                                pool.wait_ge(s_kev, s + 2)
                                spread_keys(4 * s + 4, 0)
                                spread_keys(4 * s + 5, 1)
                            if u == 3:
                                spread_keys(4 * s + 6, 2)
                                spread_keys(4 * s + 7, 3)
                        if not (last or before_last) and u == 1:
                            rstd_1(s + 2)

                with pool.Fori(0, NS - 2) as s:
                    body(s, False, False)
                body(NS - 2, True, False)
                body(NS - 1, False, True)

        x1r = sb("x1r", [P, 2, U, D])
        xn2 = sb("xn2", [P, U, D])
        stat2, mv2 = sb("stat2", [P, U, 6]), sb("mv2", [P, U, 2])
        var2, rstd2 = sb("var2", [P, U]), sb("rstd2", [P, U])
        s_x1l = [sem(f"x1_loaded{i}") for i in range(2)]
        (s_st2, s_mv2, s_va2, s_r2, s_xn2) = (sem(n) for n in (
            "ln2_bn", "ln2_stats", "ln2_var_eps", "ln2_rstd", "xn2_ready"))

        with nc.Block() as block:
            @block.sync
            def _(sp):
                def load(step, par):
                    sp.dma_start(x1r[:, par, :, :], x1_r[:, bass.ds(step * U, U), :]).then_inc(s_x1l[par], 16)

                def body(i, last):
                    for par in range(2):
                        step = 2 * i + par
                        if not last:
                            sp.wait_ge(s_xn2, step + 1)
                            load(step + 2, par)
                        sp.wait_ge(s_rte, step + 1)
                        sp.dma_start(xt2_d[:, bass.ds(step * (U * P), U * P)], xt2[:, :]).then_inc(s_rst, 16)

                for par in range(2):
                    load(par, par)
                with sp.Fori(0, NS // 2 - 1) as i:
                    body(i, False)
                body(NS // 2 - 1, True)
                sp.wait_ge(s_rst, 16 * NS)

            @block.tensor
            def _(pe):
                def transposes(step, first):
                    pe.wait_ge(s_xn2, step + 1)
                    if not first:
                        pe.wait_ge(s_rte, step)
                    for u in range(U):
                        last = nc.tensor.transpose(W0[:, u * P:(u + 1) * P], xn2[:, u, :], ident[:, :])
                    last.then_inc(s_rt, 1)

                def hidden(step, first):
                    pe.wait_ge(s_rte, step + 1)
                    if not first:
                        pe.wait_ge(s_rge, step)
                    nc.tensor.matmul(W1[0:G, :], wg1_s[:, :], xt2[:, :], start=True, stop=True).then_inc(s_rg, 1)

                def to_logits(step, first):
                    pe.wait_ge(s_rge, step + 1)
                    if not first:
                        pe.wait_ge(s_log, step)
                    for u in range(U):
                        last = nc.tensor.matmul(SA[:, u * E:(u + 1) * E], g_s[:, u * P:(u + 1) * P], wg2_s[:, :],
                                                start=True, stop=True)
                    last.then_inc(s_rl, 1)

                transposes(0, True)
                hidden(0, True)
                transposes(1, False)
                to_logits(0, True)
                with pe.Fori(1, NS - 1) as step:
                    hidden(step, False)
                    transposes(step + 1, False)
                    to_logits(step, False)
                hidden(NS - 1, False)
                to_logits(NS - 1, False)

            @block.scalar
            def _(act):
                def body(step, first):
                    act.wait_ge(s_rg, step + 1)
                    if not first:
                        act.wait_ge(s_rl, step)
                    nc.scalar.activation(g_s[:, :], W1[0:G, :], ACT.Gelu, bias=bg1_s[:, :]).then_inc(s_rge, 1)
                body(0, True)
                with act.Fori(1, NS) as step:
                    body(step, False)
                act.wait_ge(s_ch, 2)
                nc.scalar.activation(t_b[:, :, :], t_a[:, :, :], ACT.Exp).then_inc(s_rex, 1)

            @block.gpsimd
            def _(pool):
                with pool.Fori(0, NS) as step:
                    pool.wait_ge(s_mv2, step + 1)
                    nc.gpsimd.tensor_tensor(var2[:, :], mv2[:, :, 1], eps_s[:, :], ALU.add).then_inc(s_va2, 1)
                    pool.wait_ge(s_va2, step + 1)
                    nc.gpsimd.tensor_tensor(rstd2[:, :], var2[:, :], minus_half[:, :], ALU.pow).then_inc(s_r2, 1)

            @block.vector
            def _(dve):
                def stats(i, par):
                    dve.wait_ge(s_x1l[par], 16 * i + 16)
                    for u in range(U):
                        last = nc.vector.bn_stats(stat2[:, u, :], x1r[:, par, u, :])
                    last.then_inc(s_st2, 1)

                def variance():
                    for u in range(U):
                        last = nc.vector.bn_aggr(mv2[:, u, :], stat2[:, u, :])
                    last.then_inc(s_mv2, 1)

                def norm(step, par, first):
                    dve.wait_ge(s_r2, step + 1)
                    if not first:
                        dve.wait_ge(s_rt, step)
                    for u in range(U):
                        last = nc.vector.tensor_scalar(xn2[:, u, :], x1r[:, par, u, :], mv2[:, u, 0:1],
                                                       rstd2[:, u:u + 1], ALU.subtract, ALU.mult)
                    last.then_inc(s_xn2, 1)

                def evacuate(step, first):
                    dve.wait_ge(s_rt, step + 1)
                    if not first:
                        dve.wait_ge(s_rst, 16 * step)
                        dve.wait_ge(s_rg, step)
                    nc.vector.tensor_copy(xt2[:, :], W0[:, :]).then_inc(s_rte, 1)

                def keep_logits(step):
                    dve.wait_ge(s_rl, step + 1)
                    nc.vector.tensor_copy(logits[:, bass.ds(step * U, U), :],
                                          SA[:, 0:U * E].rearrange("p (u e) -> p u e", e=E)).then_inc(s_log, 1)

                stats(0, 0)
                dve.wait_ge(s_st2, 1)
                variance()
                norm(0, 0, True)
                stats(0, 1)

                def body(i, first, last):
                    for par in range(2):
                        step = 2 * i + par
                        end = last and par == 1
                        if not end:
                            dve.wait_ge(s_st2, step + 2)
                        evacuate(step, first and par == 0)
                        if not end:
                            variance()
                            norm(step + 1, 1 - par, False)
                            if not (last and par == 0):
                                stats(i + 1, par)
                        keep_logits(step)

                body(0, True, False)
                with dve.Fori(1, NS // 2 - 1) as i:
                    body(i, False, False)
                body(NS // 2 - 1, False, True)

                chain = [0]

                def link(ins):
                    chain[0] += 1
                    ins.then_inc(s_ch, 1)
                    dve.wait_ge(s_ch, chain[0])

                def wide(r):
                    return r[:, :].unsqueeze(2).broadcast_to([P, NT, E])

                iota_w = iota_e[:, :].unsqueeze(1).broadcast_to([P, NT, E])
                dve.wait_ge(s_log, NS)
                link(nc.vector.reduce_max(r_a[:, :], logits[:, :, :], AX))
                link(nc.vector.tensor_tensor(t_a[:, :, :], logits[:, :, :], wide(r_a), ALU.subtract))
                dve.wait_ge(s_rex, 1)
                link(nc.vector.reduce_sum(r_a[:, :], t_b[:, :, :], AX))
                link(nc.vector.reciprocal(r_b[:, :], r_a[:, :]))
                link(nc.vector.tensor_tensor(probs[:, :, :], t_b[:, :, :], wide(r_b), ALU.mult))
                left = probs
                for k in range(2):
                    link(nc.vector.reduce_max(r_a[:, :], left[:, :, :], AX))
                    link(nc.vector.tensor_tensor(t_a[:, :, :], left[:, :, :], wide(r_a), ALU.is_equal))
                    link(nc.vector.tensor_tensor(t_a[:, :, :], t_a[:, :, :], iota_w, ALU.mult))
                    link(nc.vector.tensor_reduce(out=r_b[:, :], in_=t_a[:, :, :], op=ALU.min, axis=AX))
                    dst = (t_b, t_a)[k]
                    link(nc.vector.tensor_tensor(dst[:, :, :], iota_w, wide(r_b), ALU.is_equal))
                    if k == 0:
                        link(nc.vector.scalar_tensor_tensor(
                            out=gates[:, :, :].rearrange("p t e -> p (t e)"),
                            in0=t_b[:, :, :].rearrange("p t e -> p (t e)"), scalar=-2.0,
                            in1=probs[:, :, :].rearrange("p t e -> p (t e)"), op0=ALU.mult, op1=ALU.add))
                        left = gates
                link(nc.vector.tensor_tensor(t_a[:, :, :], t_a[:, :, :], t_b[:, :, :], ALU.add))
                link(nc.vector.tensor_tensor(gates[:, :, :], t_a[:, :, :], probs[:, :, :], ALU.mult))

        UB = bank[0:4]
        DB = bank[4:6]

        with nc.Block() as block:
            @block.sync
            def _(sp):
                def load(step, par):
                    sp.dma_start(xt2_f[:, par, :], xt2_d[:, bass.ds(step * (U * P), U * P)]).then_inc(s_fx[par], 16)

                def load_acc(step, par):
                    sp.dma_start(acc[:, par, :, :], x1_r[:, bass.ds(step * U, U), :]).then_inc(s_fa[par], 16)

                for par in range(2):
                    load(par, par)
                    load_acc(par, par)

                def body(i, last):
                    for par in range(2):
                        step = 2 * i + par
                        if not last:
                            sp.wait_ge(s_up, 16 * step + 16)
                            load(step + 2, par)
                        sp.wait_ge(s_ac, 8 * step + 8)
                        sp.dma_start(out_r[:, bass.ds(step * U, U), :], acc[:, par, :, :]).then_inc(s_out[par], 16)
                        if not last:
                            sp.wait_ge(s_out[par], 16 * i + 16)
                            load_acc(step + 2, par)

                with sp.Fori(0, NS // 2 - 1) as i:
                    body(i, False)
                body(NS // 2 - 1, True)
                for par in range(2):
                    sp.wait_ge(s_out[par], 16 * (NS // 2))

            @block.tensor
            def _(pe):
                def up(step, par, e, first):
                    for hc in range(2):
                        n = 2 * e + hc
                        if not (first and n < 4):
                            pe.wait_ge(s_gl, 16 * step + n - 3)
                        nc.tensor.matmul(UB[n % 4][:, :], win_s[:, e, hc * P:(hc + 1) * P], xt2_f[:, par, :],
                                         start=True, stop=True).then_inc(s_up, 1)

                def down(step, e, first):
                    pe.wait_ge(s_gl, 16 * step + 2 * e + 2)
                    if not (first and e < 2):
                        pe.wait_ge(s_ac, 8 * step + e - 1)
                    for u in range(U):
                        for hc in range(2):
                            last = nc.tensor.matmul(DB[e % 2][:, u * D:(u + 1) * D],
                                                    h_s[:, (2 * e + hc) % 4, u * P:(u + 1) * P],
                                                    wout_s[:, e, hc, :], start=(hc == 0), stop=(hc == 1))
                    last.then_inc(s_dn, 1)

                def body(i, first):
                    for par in range(2):
                        step = 2 * i + par
                        now = first and par == 0
                        pe.wait_ge(s_fx[par], 16 * i + 16)
                        up(step, par, 0, now)
                        for e in range(E):
                            if e + 1 < E:
                                up(step, par, e + 1, now)
                            down(step, e, now)

                body(0, True)
                with pe.Fori(1, NS // 2) as i:
                    body(i, False)

            @block.scalar
            def _(act):
                def body(i, first):
                    for par in range(2):
                        step = 2 * i + par
                        for e in range(E):
                            for hc in range(2):
                                n = 2 * e + hc
                                act.wait_ge(s_up, 16 * step + n + 1)
                                if not (first and par == 0 and n < 4):
                                    act.wait_ge(s_dn, 8 * step + e - 1)
                                nc.scalar.activation(h_s[:, n % 4, :], UB[n % 4][:, :], ACT.Gelu).then_inc(s_gl, 1)

                body(0, True)
                with act.Fori(1, NS // 2) as i:
                    body(i, False)

            @block.vector
            def _(dve):
                def body(i, first):
                    for par in range(2):
                        step = 2 * i + par
                        nc.vector.tensor_copy(gcur[:, par, :, :], gates[:, bass.ds(step * U, U), :]).then_inc(s_gc, 1)
                        dve.wait_ge(s_gc, step + 1)
                        dve.wait_ge(s_fa[par], 16 * i + 16)
                        for e in range(E):
                            dve.wait_ge(s_dn, 8 * step + e + 1)
                            if not (first and par == 0 and e == 0):
                                dve.wait_ge(s_ac, 8 * step + e)
                            for u in range(U):
                                last = nc.vector.scalar_tensor_tensor(
                                    out=acc[:, par, u, :], in0=DB[e % 2][:, u * D:(u + 1) * D],
                                    scalar=gcur[:, par, u, e:e + 1], in1=acc[:, par, u, :],
                                    op0=ALU.mult, op1=ALU.add)
                            last.then_inc(s_ac, 1)

                body(0, True)
                with dve.Fori(1, NS // 2) as i:
                    body(i, False)


def kernel(x, ctx_1024, mask_BxS2_bk0, L0_xattn_Wq, L0_xattn_bq, L0_xattn_Wk, L0_xattn_bk, L0_xattn_Wv, L0_xattn_bv,
           L0_xattn_Wo, L0_xattn_bo, L0_ffn_wg1, L0_ffn_bg1, L0_ffn_wg2, L0_ffn_w_in, L0_ffn_w_out):
    import concourse.bacc as bacc
    from concourse.bass_utils import run_bass_kernel_spmd

    def laid(a, *shape):
        a = np.asarray(a)
        return np.ascontiguousarray(a.reshape(shape) if shape else a)

    def turned(a):
        return np.ascontiguousarray(np.asarray(a).T)

    arrays = {
        "x": laid(x, N, D),
        "ctx_t": turned(laid(ctx_1024, N, D)),
        "mask": laid(mask_BxS2_bk0),
        "wq_t": turned(L0_xattn_Wq), "bq": laid(L0_xattn_bq),
        "wk_t": turned(L0_xattn_Wk), "bk": laid(L0_xattn_bk),
        "wv_t": turned(L0_xattn_Wv), "bv": laid(L0_xattn_bv),
        "wo_t": turned(L0_xattn_Wo), "bo": laid(L0_xattn_bo),
        "wg1": laid(L0_ffn_wg1), "bg1": laid(L0_ffn_bg1), "wg2": laid(L0_ffn_wg2),
        "w_in": laid(L0_ffn_w_in), "w_out": laid(L0_ffn_w_out),
    }
    nc = bacc.Bacc("TRN2", target_bir_lowering=False, num_devices=1)
    ins = [nc.dram_tensor(n, a.shape, mybir.dt.from_np(a.dtype), kind="ExternalInput").ap() for n, a in arrays.items()]
    out = nc.dram_tensor("out", [N, D], F32, kind="ExternalOutput").ap()
    build(nc, *ins, out)
    r = run_bass_kernel_spmd(nc, [arrays], core_ids=[0])
    return r.results[0]["out"].reshape(B, L, D)
```

```python
from contextlib import ExitStack

import numpy as np

import concourse.bass as bass
from concourse import mybir

F32 = mybir.dt.float32
F16 = mybir.dt.float16
U8 = mybir.dt.uint8
U32 = mybir.dt.uint32
ALU = mybir.AluOpType
ACT = mybir.ActivationFunctionType
AX = mybir.AxisListType.X

P = 128
B, L, D = 128, 64, 128
H = 16
DH = D // H
HH = H // 2
E, HID, G = 8, 256, 32
N = B * L
NT = N // P
U = 4
NS = NT // U
SCALE = float(DH) ** -0.5
NEG = 10000000.0
EPS = 1e-5
VM = 64
J = H // 2
KTOP = 2
BT = 4
BLK = BT * P
REG = N + BLK
R3 = 3
NB = -(-((KTOP * N + E * (BLK - 1)) // BLK) // R3) * R3
RW = 140
RTOK, RGATE = D, D + 4
CH = 9


def position_encodings():
    half = D // 2
    periods = np.float32(1.0) / np.float32(10000.0) ** (np.arange(half, dtype=np.float32) / np.float32(half))
    angles = np.arange(L, dtype=np.float32)[:, None] * periods[None, :].astype(np.float32)
    return np.stack([np.sin(angles), np.cos(angles)], axis=-1).reshape(L, D).astype(np.float32)


def build(nc, x, ctxT, mask, wqT, bq, wkT, bk, wvT, bv, woT, bo, wg1, bg1, wg2, w_in, w_out, out):
    pe_c = nc.inline_tensor(np.ascontiguousarray(position_encodings().T), name="pe_t")
    ident_c = nc.inline_tensor(np.eye(P, dtype=np.float32), name="ident")
    head_of_row = (np.arange(P) % (D // 2)) // DH
    headmask_c = nc.inline_tensor((head_of_row[:, None] == np.arange(HH)[None, :]).astype(np.float32), name="headmask")
    q_of_row = np.arange(P) % L
    causal_c = nc.inline_tensor(
        np.where(np.arange(L)[None, :] > q_of_row[:, None], -NEG, 0.0).astype(np.float32), name="causal")
    ones_cols = np.zeros((P, VM), np.float32)
    for p in range(2):
        ones_cols[p * L:(p + 1) * L, 4 * DH + p] = 1.0
    ones_c = nc.inline_tensor(ones_cols, name="value_ones")
    tri_c = nc.inline_tensor((np.arange(P)[:, None] < np.arange(P)[None, :]).astype(np.float16), name="before")
    region_c = nc.inline_tensor(np.tile(np.arange(E, dtype=np.float32) * REG, (P, 1)), name="region")
    tok_c = nc.inline_tensor(
        (np.arange(U)[None, :] * P + np.arange(P)[:, None]).astype(np.uint32), name="token")
    blocks_c = nc.inline_tensor(np.tile(np.repeat(np.arange(NB, dtype=np.float32), E), (P, 1)), name="block_numbers")
    rounds_c = nc.inline_tensor(
        np.tile((np.arange(NB) - 1) // R3 + 1, (P, 1)).astype(np.float32), name="rounds_before")
    experts_c = nc.inline_tensor(np.tile(np.arange(E, dtype=np.float32), (P, 1)), name="expert_numbers")
    pad_c = np.zeros((BLK, RW), np.float32)
    pad_c[:, RTOK] = (N + np.arange(BLK)).astype(np.uint32).view(np.float32)
    pad_c = nc.inline_tensor(pad_c, name="padding_rows")
    iota_c = nc.inline_tensor(np.tile(np.arange(E, dtype=np.float32) - E, (P, 1)), name="iota_e")

    rows_d = nc.dram_tensor("routed_rows", [E * REG, RW], F32, kind="Internal").ap()

    x_r = x.rearrange("(t p) d -> p t d", p=P)
    out_r = out[0:N, :].rearrange("(t p) d -> p t d", p=P)

    with ExitStack() as ctx:
        def sb(name, shape, dt=F32):
            return ctx.enter_context(nc.sbuf_tensor(name, shape, dt))

        def sem(name):
            return ctx.enter_context(nc.semaphore(name))

        bank = [ctx.enter_context(nc.psum_tensor(f"bank{i}", [P, 512], F32)) for i in range(8)]
        W0, W1, SA, SB, PTA, PTB, XB, YB = bank
        S_bank, PT_bank = [SA, SB], [PTA, PTB]

        wq_s, wk_s, wv_s, wo_s = (sb(n, [P, D]) for n in ("wq_s", "wk_s", "wv_s", "wo_s"))
        bq_s, bk_s = sb("bq_s", [P, 1]), sb("bk_s", [P, 1])
        bv_s, bo_s = sb("bv_s", [P, 1]), sb("bo_s", [P, D])
        bvb_s, cvec = sb("bvb_s", [P, P]), sb("cvec", [P, D])
        pe_s, ident = sb("pe_s", [P, L]), sb("ident_s", [P, P])
        headmask, causal = sb("headmask_s", [P, HH]), sb("causal_s", [P, L])
        iota_e = sb("iota_e_s", [P, E])
        ones_s = sb("ones_s", [P, VM])
        wg1_s, bg1_s, wg2_s = sb("wg1_s", [D, G]), sb("bg1_s", [G, 1]), sb("wg2_s", [G, E])
        tri_s, ones16 = sb("tri_s", [P, P], F16), sb("ones16", [P, P], F16)
        run_s, tok_s = sb("run_s", [P, E]), sb("tok_s", [P, U], U32)
        region_s = sb("region_s", [P, E])
        blocks_s, experts_s = sb("blocks_s", [P, NB, E]), sb("experts_s", [P, E])
        rounds_s = sb("rounds_s", [P, NB])
        pad_s = sb("pad_s", [P, BT, RW])

        x_in = sb("x_in", [P, U, D])
        ctx_k = sb("ctx_k", [P, U * P])
        ctx_v = sb("ctx_v", [P, U * P])
        mask_in = sb("mask_in", [P, U, L], U8)
        negmask = sb("negmask", [P, U, L])
        x_res = sb("x_res", [P, U, D])
        stat1, mv1, rstd1 = sb("stat1", [P, U, 6]), sb("mv1", [P, U, 2]), sb("rstd1", [P, U])
        xn = sb("xn", [P, U, D])
        minus_half, eps_s = sb("minus_half", [P, U]), sb("eps_s", [P, U])
        step_u, zero_u = sb("step_u", [P, U], U32), sb("zero_u", [P, U], U32)
        minus_one = sb("minus_one", [P, U])
        var1, shift1 = sb("var1", [P, U]), sb("shift1", [P, U])
        xT = sb("xT", [P, U * P])
        q2 = sb("q2", [P, 2, 2, U, P])
        k2 = sb("k2", [P, 2, 2, U, L])
        kx = sb("kx", [P, U, 2, HH, L])
        vx = sb("vx", [P, U, J, VM])
        sm = sb("sm", [P, 2, H, L])
        smax = sb("smax", [P, H])
        pt = sb("pt", [P, J, P])
        xo = sb("xo", [P, 4, P])
        rden = sb("rden", [P, J, 2])
        on = sb("on", [P, D])
        onT = sb("onT", [P, P])
        x1 = sb("x1", [P, 2, U, D])

        stat2, mv2 = sb("stat2", [P, U, 6]), sb("mv2", [P, U, 2])
        var2, rstd2, shift2 = sb("var2", [P, U]), sb("rstd2", [P, U]), sb("shift2", [P, U])
        rows = sb("rows", [P, 2, U, RW])
        xt2 = sb("xt2", [P, U * P])
        hid_s = sb("hid_s", [G, U * P])
        lg, ex, probs, left = (sb(n, [P, U, E]) for n in ("lg", "ex", "probs", "left"))
        largest, two_largest = sb("largest", [P, U, 8]), sb("two_largest", [P, U, 8])
        r_max, r_sum, r_inv = (sb(n, [P, U]) for n in ("r_max", "r_sum", "r_inv"))
        sel16 = sb("sel16", [P, U, E], F16)
        rank = sb("rank", [P, U, E])
        pos_f = sb("pos_f", [P, KTOP, U])
        pos = sb("pos", [P, 2, KTOP, U], U32)
        (s_st2, s_mv2, s_va2, s_r2, s_xn2, s_rt, s_rte, s_rg, s_rge, s_rl, s_lg, s_lsh, s_rex, s_ch, s_sel, s_rank,
         s_pos, s_tokadd, s_tok, s_gate, s_pch, s_left, s_two) = (sem(n) for n in (
             "ln2_bn", "ln2_stats", "ln2_var_eps", "ln2_rstd", "rows_normed", "xn2_transposed", "xt2_ready",
             "hidden_in_psum", "hidden_ready", "logits_in_psum", "logits_copied", "logits_shifted", "logits_exp",
             "routing_chain", "selection_ready", "rank_in_psum", "positions_ready", "token_counted", "token_written",
             "gates_written", "positions_chain", "two_largest_replaced", "two_largest_filled"))
        s_scat = [sem(f"rows_scattered{i}") for i in range(2)]

        s_w, s_x, s_ck, s_cv, s_m = (sem(n) for n in ("weights_in", "x_loaded", "ctx_k_loaded", "ctx_v_loaded", "mask_loaded"))
        s_xr = [sem(f"x_res_loaded{u}") for u in range(U)]
        s_x1st = [[sem(f"x1_stored{i}{u}") for u in range(U)] for i in range(2)]
        (s_zero, s_stat, s_xn, s_cp, s_neg, s_xt, s_xTs, s_k, s_kev, s_q, s_qev, s_v, s_vev, s_kx,
         s_sc, s_stt, s_max, s_sub, s_exp, s_pt, s_ptev, s_pv, s_xev, s_tq, s_rden, s_norm, s_ont,
         s_ontev, s_y, s_xres, s_res, s_bvb, s_cv, s_cvec, s_r1, s_st1, s_cv_ps, s_va1, s_mh) = (sem(n) for n in (
             "zeroed", "ln1_stats", "xn_ready", "ctx_k_ready", "negmask_ready", "xT_in_psum", "xT_ready",
             "k_in_psum", "k2_ready", "q_in_psum", "q2_ready", "v_in_psum", "vx_ready", "kx_ready",
             "scores_in_psum", "scores_masked", "row_max", "scores_shifted", "probs_ready", "pt_in_psum",
             "pt_ready", "pv_in_psum", "xo_ready", "o_in_psum", "rden_ready", "o_normed", "onT_in_psum",
             "onT_ready", "y_in_psum", "x_res_ready", "x1_ready",
             "bv_spread", "cvec_in_psum", "cvec_ready", "ln1_rstd", "ln1_bn", "bias_in_psum",
             "ln1_var_eps", "minus_half_set"))
        NW = 24

        count = sb("count", [P, E])
        blocks_of, ends = sb("blocks_of", [P, E]), sb("ends", [P, E])
        past, skipped = sb("past", [P, NB, E]), sb("skipped", [P, NB, E])
        of_block = sb("of_block", [P, NB])
        start_of = sb("start_of", [P, NB])
        active, row_f = sb("active", [P, NB]), sb("row_f", [P, NB])
        same = sb("same", [P, NB])
        expert_oh = sb("expert_oh", [P, NB, E])
        table = sb("table", [P, 3, NB], U32)
        tails = sb("tails", [P, E], U32)

        wi, wo = sb("wi", [P, R3, HID]), sb("wo", [P, E, 2, D])
        xb = sb("xb", [P, R3, BT, RW])
        xbT = sb("xbT", [P, R3, BLK])
        hb = sb("hb", [P, R3, 2, BLK])
        gtmp, gate = sb("gtmp", [P, BT, E]), sb("gate", [P, R3, BT])
        token = sb("token_ids", [P, R3, BT], U32)
        yb = sb("yb", [P, R3, BT, D])
        s_tab, s_tabd, s_tails, s_padl, s_init, s_tail, s_wo = (sem(n) for n in (
            "table_chain", "table_ready", "tails_ready", "padding_loaded", "dummy_rows_zeroed", "padding_stored",
            "w_out_loaded"))
        s_xb = [sem(f"rows_loaded{i}") for i in range(R3)]
        s_wi = [sem(f"w_in_loaded{i}") for i in range(R3)]
        s_add = [sem(f"added_to_out{i}") for i in range(R3)]
        (s_bt, s_bte, s_up, s_gl, s_dn, s_gm, s_gt, s_tk, s_yb) = (sem(n) for n in (
            "block_transposed", "xbT_ready", "up_in_psum", "gelu_ready", "down_in_psum", "gate_masked", "gate_picked",
            "token_copied", "yb_ready"))
        TBK, UBK, DBK = bank[0:3], bank[3:5], bank[5:8]

        def runs(s, lo=0, hi=NS - 1):
            return not isinstance(s, int) or lo <= s <= hi

        with nc.Block() as block:

            @block.sync
            def _(sp):
                for dst, src in ((wq_s[:, :], wqT), (wk_s[:, :], wkT), (wv_s[:, :], wvT), (wo_s[:, :], woT),
                                 (bq_s[:, :], bq.rearrange("(p a) -> p a", a=1)),
                                 (bk_s[:, :], bk.rearrange("(p a) -> p a", a=1)),
                                 (bv_s[:, :], bv.rearrange("(p a) -> p a", a=1)),
                                 (bo_s[:, :], bo.partition_broadcast(P)),
                                 (pe_s[:, :], pe_c.ap()), (ident[:, :], ident_c.ap()),
                                 (headmask[:, :], headmask_c.ap()), (causal[:, :], causal_c.ap()),
                                 (iota_e[:, :], iota_c.ap()), (ones_s[:, :], ones_c.ap()),
                                 (wg1_s[:, :], wg1), (bg1_s[:, :], bg1.rearrange("(p a) -> p a", a=1)),
                                 (wg2_s[:, :], wg2), (tri_s[:, :], tri_c.ap()), (run_s[:, :], region_c.ap()),
                                 (region_s[:, :], region_c.ap()), (tok_s[:, :], tok_c.ap()),
                                 (blocks_s[:, :, :].rearrange("p b e -> p (b e)"), blocks_c.ap()),
                                 (experts_s[:, :], experts_c.ap()), (rounds_s[:, :], rounds_c.ap())):
                    sp.dma_start(dst, src).then_inc(s_w, 16)

                def load_x(s):
                    sp.dma_start(x_in[:, :, :], x_r[:, bass.ds(s * U, U), :]).then_inc(s_x, 16)

                def load_ctx_k(s):
                    sp.dma_start(ctx_k[:, :], ctxT[:, bass.ds(s * (U * P), U * P)]).then_inc(s_ck, 16)

                def load_ctx_v(s):
                    sp.dma_start(ctx_v[:, :], ctxT[:, bass.ds(s * (U * P), U * P)]).then_inc(s_cv, 16)

                def load_mask(s):
                    for b in range(2):
                        src = mask[bass.ds(s * (2 * U), 2 * U), :].rearrange("(u b) k -> b u k", b=2)[b]
                        sp.dma_start(mask_in[b * L:(b + 1) * L, :, :], src.partition_broadcast(L)).then_inc(s_m, 16)

                def load_x_res(s, u):
                    sp.dma_start(x_res[:, u, :], x_r[:, bass.ds(s * U + u, 1), :].rearrange("p a d -> p (a d)")
                                 ).then_inc(s_xr[u], 16)

                def store_tile(s, i, par, u):
                    t = s * U + u
                    sp.wait_ge(s_res, t + 1)
                    sp.dma_start(out_r[:, bass.ds(t, 1), :].rearrange("p a d -> p (a d)"), x1[:, par, u, :]
                                 ).then_inc(s_x1st[par][u], 16)

                load_x(0)
                load_ctx_k(0)
                load_ctx_v(0)
                load_mask(0)
                for u in range(U):
                    load_x_res(0, u)
                sp.dma_start(pad_s[:, :, :], pad_c.ap().rearrange("(u p) w -> p u w", p=P)).then_inc(s_padl, 16)
                sp.wait_ge(s_xn, 1)
                load_x(1)
                sp.wait_ge(s_k, 1)
                load_ctx_k(1)
                sp.wait_ge(s_v, 1)
                load_ctx_v(1)
                sp.wait_ge(s_neg, 1)
                load_mask(1)
                sp.wait_ge(s_xn, 2)
                load_x(2)
                sp.wait_ge(s_k, 2)
                load_ctx_k(2)
                sp.dma_start(wo[:, :, :, :].rearrange("p e c d -> p (e c) d"),
                             w_out.rearrange("e (c p) d -> p (e c) d", p=P)).then_inc(s_wo, 16)
                sp.wait_ge(s_padl, 16)

                def body(s, i, par):
                    for u in range(U):
                        if u == 2 and runs(s, 0, NS - 3):
                            sp.wait_ge(s_neg, s + 2)
                            load_mask(s + 2)
                        if u == 3 and runs(s, 0, NS - 4):
                            sp.wait_ge(s_k, s + 3)
                            load_ctx_k(s + 3)
                            sp.wait_ge(s_xn, s + 3)
                            load_x(s + 3)
                        if u == 3 and runs(s, 0, NS - 3):
                            sp.wait_ge(s_v, s + 2)
                            load_ctx_v(s + 2)
                        if u or runs(s, 1):
                            ps, ppar, pu = (s, par, u - 1) if u else (s - 1, 1 - par, U - 1)
                            store_tile(ps, i, ppar, pu)
                            if u == 0 or runs(s, 0, NS - 2):
                                load_x_res(ps + 1, pu)

                for s in range(4):
                    body(s, s // 2, s % 2)
                with sp.Fori(2, NS // 2 - 2) as i:
                    for par in range(2):
                        body(2 * i + par, i, par)
                for s in range(NS - 4, NS):
                    body(s, s // 2, s % 2)
                store_tile(NS - 1, NS // 2 - 1, 1, U - 1)
                for par in range(2):
                    for u in range(U):
                        sp.wait_ge(s_x1st[par][u], 16 * (NS // 2))

                def pad_region(e):
                    at = nc.values_load(tails[0:1, e:e + 1], engines=[mybir.EngineType.SP], min_val=e * REG,
                                        max_val=e * REG + N)
                    sp.dma_start(rows_d[bass.ds(at, BLK), :].rearrange("(u p) w -> p u w", p=P), pad_s[:, :, :]
                                 ).then_inc(s_tail, 16)

                def load_block(b, r):
                    expert = nc.values_load(table[0:1, 1, bass.ds(b, 1)], engines=[mybir.EngineType.SP],
                                            min_val=0, max_val=E - 1)
                    at = nc.values_load(table[0:1, 0, bass.ds(b, 1)], engines=[mybir.EngineType.SP],
                                        min_val=0, max_val=E * REG - BLK)
                    if not (isinstance(b, int) and b < R3):
                        sp.wait_ge(s_bt, b - R3 + 1)
                        sp.wait_ge(s_tk, b - R3 + 1)
                        sp.wait_ge(s_gm, b - R3 + 1)
                    sp.dma_start(xb[:, r, :, :], rows_d[bass.ds(at, BLK), :].rearrange("(u p) w -> p u w", p=P)
                                 ).then_inc(s_xb[r], 16)
                    if not (isinstance(b, int) and b < R3):
                        sp.wait_ge(s_up, 2 * (b - R3 + 1))
                    sp.dma_start(wi[:, r, :], w_in[bass.ds(expert, 1), :, :].rearrange("e d h -> d (e h)")
                                 ).then_inc(s_wi[r], 16)

                sp.dma_start(out[N:N + BLK, :].rearrange("(u p) d -> p u d", p=P), pad_s[:, :, 0:D]).then_inc(s_init, 16)
                sp.wait_ge(s_tails, 1)
                for e in range(E // 2):
                    pad_region(e)
                sp.wait_ge(s_tabd, 1)
                sp.wait_ge(s_tail, 16 * E)
                for par in range(2):
                    sp.wait_ge(s_scat[par], 16 * KTOP * U * (NS // 2))
                for b in range(R3):
                    load_block(b, b)
                with sp.Fori(1, NB // R3) as i:
                    for r in range(R3):
                        load_block(R3 * i + r, r)


            @block.tensor
            def _(pe):
                def t_x(s):
                    pe.wait_ge(s_xn, s + 1)
                    for u in range(U):
                        last = nc.tensor.transpose(W0[:, u * P:(u + 1) * P], xn[:, u, :], ident[:, :])
                    last.then_inc(s_xt, 1)

                def project_k(s):
                    pe.wait_ge(s_cp, s + 1)
                    nc.tensor.matmul(W1[:, :], wk_s[:, :], ctx_k[:, :], start=True, stop=True).then_inc(s_k, 1)

                def project_q(s):
                    pe.wait_ge(s_xTs, s + 1)
                    nc.tensor.matmul(W0[:, :], wq_s[:, :], xT[:, :], start=True, stop=True).then_inc(s_q, 1)

                def project_v(s):
                    pe.wait_ge(s_cv, 16 * (s + 1))
                    pe.wait_ge(s_qev, s + 1)
                    for u in range(U):
                        last = nc.tensor.matmul(W0[:, u * P:(u + 1) * P], ctx_v[:, u * P:(u + 1) * P], wv_s[:, :],
                                                start=True, stop=True)
                    last.then_inc(s_v, 1)

                def scores(t, u, par):
                    pe.wait_ge(s_kx, t + 1)
                    for half in range(2):
                        nc.tensor.matmul(S_bank[half][:, :], q2[:, par, half, u, :],
                                         kx[:, u, half, :, :].rearrange("p h k -> p (h k)"),
                                         start=True, stop=True).then_inc(s_sc, 1)

                def transpose_probs(t, u):
                    pe.wait_ge(s_exp, t + 1)
                    pr = sm[:, u % 2, :, :].rearrange("p h k -> p (h k)")
                    for j in range(J):
                        last = nc.tensor.transpose(PT_bank[j // 4][:, (j % 4) * P:(j % 4 + 1) * P],
                                                   pr[:, j * P:(j + 1) * P], ident[:, :])
                        if j % 4 == 3:
                            last.then_inc(s_pt, 1)

                def values(t, u):
                    pe.wait_ge(s_ptev, 2 * t + 2)
                    for j in range(J):
                        o = VM * (j % 2)
                        last = nc.tensor.matmul(XB[o:o + VM, (j // 2) * P:(j // 2 + 1) * P], vx[:, u, j, :],
                                                pt[:, j, :], start=True, stop=True)
                    last.then_inc(s_pv, 1)

                def queries_to_rows(t):
                    pe.wait_ge(s_xev, t + 1)
                    for c in range(4):
                        last = nc.tensor.transpose(YB[:, c * P:(c + 1) * P], xo[:, c, :], ident[:, :])
                    last.then_inc(s_tq, 1)

                def transpose_o(t):
                    pe.wait_ge(s_norm, t + 1)
                    nc.tensor.transpose(YB[:, 0:P], on[:, :], ident[:, :]).then_inc(s_ont, 1)

                def project_o(t):
                    pe.wait_ge(s_ontev, t + 1)
                    nc.tensor.matmul(YB[:, P:2 * P], onT[:, :], wo_s[:, :], start=True, stop=True).then_inc(s_y, 1)

                pe.wait_ge(s_w, 16 * NW)
                pe.wait_ge(s_bvb, 1)
                nc.tensor.matmul(YB[:, 0:D], bvb_s[:, :], wo_s[:, :], start=True, stop=True).then_inc(s_cv_ps, 1)
                t_x(0)
                project_k(0)
                project_q(0)
                pe.wait_ge(s_zero, 4)
                pe.wait_ge(s_qev, 1)
                scores(0, 0, 0)
                pe.wait_ge(s_kev, 1)
                project_k(1)
                project_v(0)
                pe.wait_ge(s_stt, 2)
                scores(1, 1, 0)
                pe.wait_ge(s_cvec, 1)

                def transpose_rows(r, par):
                    pe.wait_ge(s_xn2, r + 1)
                    for u in range(U):
                        last = nc.tensor.transpose(W1[:, u * P:(u + 1) * P], rows[:, par, u, 0:D], ident[:, :])
                    last.then_inc(s_rt, 1)

                def gate_hidden(r):
                    pe.wait_ge(s_rte, r + 1)
                    nc.tensor.matmul(W1[0:G, :], wg1_s[:, :], xt2[:, :], start=True, stop=True).then_inc(s_rg, 1)

                def gate_logits(r):
                    pe.wait_ge(s_rge, r + 1)
                    for u in range(U):
                        last = nc.tensor.matmul(YB[:, 256 + u * E:256 + (u + 1) * E], hid_s[:, u * P:(u + 1) * P],
                                                wg2_s[:, :], start=True, stop=True)
                    last.then_inc(s_rl, 1)

                def rank_tokens(r):
                    pe.wait_ge(s_sel, r + 1)
                    o, n = 288, 288 + U * E
                    nc.tensor.matmul(YB[:, o:n], tri_s[:, :], sel16[:, :, :].rearrange("p u e -> p (u e)"),
                                     start=True, stop=False, skip_group_check=True)
                    for k in range(1, U):
                        nc.tensor.matmul(YB[:, o + k * E:n], ones16[:, :],
                                         sel16[:, 0:U - k, :].rearrange("p u e -> p (u e)"),
                                         start=False, stop=False, skip_group_check=True)
                    for u in range(U):
                        last = nc.tensor.matmul(YB[:, n:n + E], ones16[:, :], sel16[:, u, :],
                                                start=False, stop=(u == U - 1), skip_group_check=True)
                    last.then_inc(s_rank, 1)

                def body(s, i, par):
                    for u in range(U):
                        t = s * U + u
                        before = u or runs(s, 1)
                        transpose_probs(t, u)
                        if before:
                            if u > 1 or runs(s, 1):
                                pe.wait_ge(s_res, t - 1)
                            if u == 2 and runs(s, 2):
                                pe.wait_ge(s_lg, s - 1)
                            if u == 0 and runs(s, 3):
                                pe.wait_ge(s_pos, s - 2)
                            queries_to_rows(t - 1)
                        if u == 0 and runs(s, 0, NS - 2):
                            pe.wait_ge(s_vev, s + 1)
                            t_x(s + 1)
                        if u == 1 and runs(s, 0, NS - 2):
                            project_q(s + 1)
                        if u == 2 and runs(s, 0, NS - 3):
                            pe.wait_ge(s_kev, s + 2)
                            if runs(s, 2):
                                pe.wait_ge(s_rge, s - 1)
                            project_k(s + 2)
                        if u < 2 or runs(s, 0, NS - 2):
                            pe.wait_ge(s_stt, 2 * t + 4)
                            if u == 2:
                                pe.wait_ge(s_qev, s + 2)
                            scores(t + 2, (u + 2) % U, par if u < 2 else 1 - par)
                        if u == 0 and runs(s, 2):
                            if runs(s, 0, NS - 2):
                                pe.wait_ge(s_kev, s + 2)
                            transpose_rows(s - 2, par)
                        if before:
                            transpose_o(t - 1)
                        if u == 3 and runs(s, 0, NS - 2):
                            project_v(s + 1)
                        if before:
                            pe.wait_ge(s_ontev, t)
                            if u == 1 and runs(s, 2):
                                gate_logits(s - 2)
                            if u == 3 and runs(s, 2):
                                rank_tokens(s - 2)
                            project_o(t - 1)
                        if u == 0:
                            pe.wait_ge(s_vev, s + 1)
                        values(t, u)
                        if u == 0 and runs(s, 2):
                            gate_hidden(s - 2)

                for s in range(4):
                    body(s, s // 2, s % 2)
                with pe.Fori(2, NS // 2 - 2) as i:
                    for par in range(2):
                        body(2 * i + par, i, par)
                for s in range(NS - 4, NS):
                    body(s, s // 2, s % 2)
                pe.wait_ge(s_res, NT - 1)
                pe.wait_ge(s_pos, NS - 2)
                queries_to_rows(NT - 1)
                transpose_o(NT - 1)
                project_o(NT - 1)
                transpose_rows(NS - 2, 0)
                gate_hidden(NS - 2)
                pe.wait_ge(s_res, NT)
                gate_logits(NS - 2)
                pe.wait_ge(s_rge, NS - 1)
                transpose_rows(NS - 1, 1)
                gate_hidden(NS - 1)
                pe.wait_ge(s_lg, NS - 1)
                rank_tokens(NS - 2)
                pe.wait_ge(s_pos, NS - 1)
                gate_logits(NS - 1)
                pe.wait_ge(s_lg, NS)
                rank_tokens(NS - 1)

                def expert_of(b):
                    return nc.values_load(table[0:1, 1, bass.ds(b, 1)], engines=[mybir.EngineType.PE],
                                          min_val=0, max_val=E - 1)

                def transposes(b, i, r):
                    pe.wait_ge(s_xb[r], 16 * i + 16)
                    if not (isinstance(b, int) and b < R3):
                        pe.wait_ge(s_bte, b - R3 + 1)
                    for u in range(BT):
                        last = nc.tensor.transpose(TBK[r][:, u * P:(u + 1) * P], xb[:, r, u, 0:D], ident[:, :])
                    last.then_inc(s_bt, 1)

                def up(b, i, r, first=False):
                    pe.wait_ge(s_wi[r], 16 * i + 16)
                    pe.wait_ge(s_bte, b + 1)
                    if not first:
                        pe.wait_ge(s_gl, 2 * b)
                    for c in range(2):
                        nc.tensor.matmul(UBK[c][:, 0:BLK],
                                         wi[:, r, c * P:(c + 1) * P],
                                         xbT[:, r, :], start=True, stop=True).then_inc(s_up, 1)

                def down(b, r):
                    e = expert_of(b)
                    pe.wait_ge(s_gl, 2 * b + 2)
                    if not (isinstance(b, int) and b < R3):
                        pe.wait_ge(s_yb, b - R3 + 1)
                    for u in range(BT):
                        for c in range(2):
                            last = nc.tensor.matmul(DBK[r][:, u * D:(u + 1) * D], hb[:, r, c, u * P:(u + 1) * P],
                                                    wo[:, bass.ds(e, 1), c, :].rearrange("p e d -> p (e d)"),
                                                    start=(c == 0), stop=(c == 1))
                    last.then_inc(s_dn, 1)

                pe.wait_ge(s_wo, 16)
                pe.wait_ge(s_tabd, 1)
                transposes(0, 0, 0)
                transposes(1, 0, 1)
                up(0, 0, 0, True)
                for b in range(R3):
                    up(b + 1, (b + 1) // R3, (b + 1) % R3)
                    transposes(b + 2, (b + 2) // R3, (b + 2) % R3)
                    down(b, b)
                with pe.Fori(1, NB // R3 - 1) as i:
                    for r in range(R3):
                        b = R3 * i + r
                        up(b + 1, i + (r + 1) // R3, (r + 1) % R3)
                        transposes(b + 2, i + (r + 2) // R3, (r + 2) % R3)
                        down(b, r)
                for r in range(R3):
                    b = NB - R3 + r
                    if r < R3 - 1:
                        up(b + 1, NB // R3 - 1, r + 1)
                    if r < R3 - 2:
                        transposes(b + 2, NB // R3 - 1, r + 2)
                    down(b, r)


            @block.scalar
            def _(act):
                def k_evac(s, par):
                    act.wait_ge(s_k, s + 1)
                    src = W1[:, :].rearrange("c (u b k) -> c u b k", u=U, b=2)
                    for half in range(2):
                        r = slice(half * 64, half * 64 + 64)
                        for b in range(2):
                            last = nc.scalar.activation(k2[b * 64:b * 64 + 64, par, half, :, :], src[r, :, b, :],
                                                        ACT.Identity, bias=bk_s[r, :])
                    last.then_inc(s_kev, 1)

                def q_evac(s, par):
                    act.wait_ge(s_q, s + 1)
                    src = W0[:, :].rearrange("c (u b k) -> c u b k", u=U, b=2)
                    for half in range(2):
                        r = slice(half * 64, half * 64 + 64)
                        for b in range(2):
                            last = nc.scalar.activation(q2[b * 64:b * 64 + 64, par, half, :, b * L:(b + 1) * L],
                                                        src[r, :, b, :], ACT.Identity, bias=bq_s[r, :])
                    last.then_inc(s_qev, 1)

                def v_evac(s):
                    act.wait_ge(s_v, s + 1)
                    src = W0[:, :].rearrange("r (uj p c) -> r uj p c", p=2, c=DH)
                    dst = vx[:, :, :, :].rearrange("r u j m -> r (u j) m")
                    for b in range(2):
                        for p in range(2):
                            o = (2 * b + p) * DH
                            last = nc.scalar.activation(dst[p * 64:p * 64 + 64, :, o:o + DH],
                                                        src[b * 64:b * 64 + 64, :, p, :], ACT.Copy)
                    last.then_inc(s_vev, 1)

                def exps(t, u):
                    act.wait_ge(s_sub, t + 1)
                    nc.scalar.activation(sm[:, u % 2, :, :], sm[:, u % 2, :, :], ACT.Exp).then_inc(s_exp, 1)

                def onT_evac(t):
                    act.wait_ge(s_ont, t + 1)
                    nc.scalar.activation(onT[:, :], YB[:, 0:P], ACT.Copy).then_inc(s_ontev, 1)

                act.wait_ge(s_w, 16 * NW)
                def ln1_norm(s):
                    act.wait_ge(s_r1, s + 1)
                    for u in range(U):
                        last = nc.scalar.activation(xn[:, u, :], x_in[:, u, :], ACT.Identity,
                                                    bias=shift1[:, u:u + 1], scale=rstd1[:, u:u + 1])
                    last.then_inc(s_xn, 1)

                def ln2_norm(r, ir, par):
                    if runs(r, 2):
                        act.wait_ge(s_scat[par], 16 * KTOP * U * ir)
                    act.wait_ge(s_r2, r + 1)
                    for u in range(U):
                        last = nc.scalar.activation(rows[:, par, u, 0:D], x1[:, par, u, :], ACT.Identity,
                                                    bias=shift2[:, u:u + 1], scale=rstd2[:, u:u + 1])
                    last.then_inc(s_xn2, 1)

                act.wait_ge(s_zero, 4)
                ln1_norm(0)
                k_evac(0, 0)
                q_evac(0, 0)
                act.wait_ge(s_xt, 1)
                ln1_norm(1)
                k_evac(1, 1)
                v_evac(0)
                exps(0, 0)

                def xt2_evac(r):
                    act.wait_ge(s_rt, r + 1)
                    nc.scalar.activation(xt2[:, :], W1[:, :], ACT.Copy).then_inc(s_rte, 1)

                def gate_gelu(r):
                    act.wait_ge(s_rg, r + 1)
                    if runs(r, 1):
                        act.wait_ge(s_rl, r)
                    nc.scalar.activation(hid_s[:, :], W1[0:G, :], ACT.Gelu, bias=bg1_s[:, :]).then_inc(s_rge, 1)

                def gate_exp(r):
                    act.wait_ge(s_lsh, r + 1)
                    nc.scalar.activation(ex[:, :, :], lg[:, :, :], ACT.Exp).then_inc(s_rex, 1)

                def body(s, i, par):
                    for u in range(U):
                        t = s * U + u
                        for c in range(2):
                            act.wait_ge(s_pt, 2 * t + c + 1)
                            nc.scalar.activation(pt[:, 4 * c:4 * c + 4, :].rearrange("p j q -> p (j q)"),
                                                 PT_bank[c][:, :], ACT.Copy).then_inc(s_ptev, 1)
                        if u == 2 and runs(s, 0, NS - 3):
                            act.wait_ge(s_kx, 4 * s + 4)
                            k_evac(s + 2, par)
                        if u or runs(s, 1):
                            onT_evac(t - 1)
                        if u == 0 and runs(s, 2):
                            xt2_evac(s - 2)
                        if u < U - 1 or runs(s, 0, NS - 2):
                            exps(t + 1, u + 1)
                        if u == 1 and runs(s, 0, NS - 2):
                            q_evac(s + 1, 1 - par)
                        act.wait_ge(s_pv, t + 1)
                        nc.scalar.activation(xo[:, :, :].rearrange("p c q -> p (c q)"), XB[:, :], ACT.Copy
                                             ).then_inc(s_xev, 1)
                        if u == 0 and runs(s, 2):
                            gate_gelu(s - 2)
                        if u == 1 and runs(s, 2):
                            gate_exp(s - 2)
                        if u == 2 and runs(s, 0, NS - 3):
                            act.wait_ge(s_xt, s + 2)
                            ln1_norm(s + 2)
                        if u == 3 and runs(s, 0, NS - 2):
                            v_evac(s + 1)
                        if u == 3 and runs(s, 1):
                            ln2_norm(s - 1, i - 1 + par, 1 - par)

                for s in range(4):
                    body(s, s // 2, s % 2)
                with act.Fori(2, NS // 2 - 2) as i:
                    for par in range(2):
                        body(2 * i + par, i, par)
                for s in range(NS - 4, NS):
                    body(s, s // 2, s % 2)
                onT_evac(NT - 1)
                xt2_evac(NS - 2)
                gate_gelu(NS - 2)
                ln2_norm(NS - 1, NS // 2 - 1, 1)
                xt2_evac(NS - 1)
                gate_gelu(NS - 1)
                gate_exp(NS - 2)
                gate_exp(NS - 1)

                def pad_region(e):
                    at = nc.values_load(tails[0:1, e:e + 1], engines=[mybir.EngineType.Activation], min_val=e * REG,
                                        max_val=e * REG + N)
                    act.dma_start(rows_d[bass.ds(at, BLK), :].rearrange("(u p) w -> p u w", p=P), pad_s[:, :, :]
                                  ).then_inc(s_tail, 16)

                def xbT_evac(b, r):
                    act.wait_ge(s_bt, b + 1)
                    if not (isinstance(b, int) and b < R3):
                        act.wait_ge(s_up, 2 * (b - R3 + 1))
                    nc.scalar.activation(xbT[:, r, :], TBK[r][:, 0:BLK], ACT.Copy).then_inc(s_bte, 1)

                def gelus(b, r):
                    for c in range(2):
                        act.wait_ge(s_up, 2 * b + c + 1)
                        if not (isinstance(b, int) and b < R3):
                            act.wait_ge(s_dn, b - R3 + 1)
                        nc.scalar.activation(hb[:, r, c, :], UBK[c][:, 0:BLK], ACT.Gelu).then_inc(s_gl, 1)

                act.wait_ge(s_padl, 16)
                act.wait_ge(s_tails, 1)
                for e in range(E // 2, E):
                    pad_region(e)
                xbT_evac(0, 0)
                xbT_evac(1, 1)
                gelus(0, 0)
                for b in range(R3):
                    gelus(b + 1, (b + 1) % R3)
                    xbT_evac(b + 2, (b + 2) % R3)
                with act.Fori(1, NB // R3 - 1) as i:
                    for r in range(R3):
                        gelus(R3 * i + r + 1, (r + 1) % R3)
                        xbT_evac(R3 * i + r + 2, (r + 2) % R3)
                for r in range(R3):
                    if r < R3 - 1:
                        gelus(NB - R3 + r + 1, r + 1)
                    if r < R3 - 2:
                        xbT_evac(NB - R3 + r + 2, r + 2)

            @block.vector
            def _(dve):
                def ln1_stats(s):
                    dve.wait_ge(s_x, 16 * (s + 1))
                    for u in range(U):
                        last = nc.vector.bn_stats(stat1[:, u, :], x_in[:, u, :])
                    last.then_inc(s_st1, 1)

                def ln1_variance():
                    for u in range(U):
                        last = nc.vector.bn_aggr(mv1[:, u, :], stat1[:, u, :])
                    last.then_inc(s_stat, 1)

                def x_evac(s):
                    dve.wait_ge(s_xt, s + 1)
                    nc.vector.tensor_tensor(xT[:, :].rearrange("p (b k) -> p b k", k=L),
                                            W0[:, :].rearrange("p (b k) -> p b k", k=L),
                                            pe_s[:, :].unsqueeze(1).broadcast_to([P, 2 * U, L]), ALU.add
                                            ).then_inc(s_xTs, 1)

                def make_mask(s):
                    dve.wait_ge(s_m, 32 * (s + 1))
                    nc.vector.scalar_tensor_tensor(out=negmask[:, :, :], in0=mask_in[:, :, :], scalar=-NEG,
                                                   in1=causal[:, :].unsqueeze(1).broadcast_to([P, U, L]),
                                                   op0=ALU.mult, op1=ALU.min).then_inc(s_neg, 1)

                def mask_scores(t, u):
                    for half in range(2):
                        dve.wait_ge(s_sc, 2 * t + half + 1)
                        nc.vector.scalar_tensor_tensor(
                            out=sm[:, u % 2, half * HH:(half + 1) * HH, :],
                            in0=S_bank[half][:, :].rearrange("p (h k) -> p h k", k=L), scalar=SCALE,
                            in1=negmask[:, u, :].unsqueeze(1).broadcast_to([P, HH, L]),
                            op0=ALU.mult, op1=ALU.add).then_inc(s_stt, 1)

                def shift_scores(t, u):
                    dve.wait_ge(s_stt, 2 * t + 2)
                    nc.vector.reduce_max(smax[:, :], sm[:, u % 2, :, :], AX).then_inc(s_max, 1)
                    dve.wait_ge(s_max, t + 1)
                    nc.vector.tensor_tensor(sm[:, u % 2, :, :], sm[:, u % 2, :, :],
                                            smax[:, :].unsqueeze(2).broadcast_to([P, H, L]),
                                            ALU.subtract).then_inc(s_sub, 1)

                def normalise(t):
                    dve.wait_ge(s_tq, t + 1)
                    y = YB[:, :].rearrange("r (j m) -> r j m", m=VM)
                    nc.vector.reciprocal(rden[:, :, :], y[:, :, 4 * DH:4 * DH + 2]).then_inc(s_rden, 1)
                    dve.wait_ge(s_rden, t + 1)
                    for b in range(2):
                        r = slice(b * 64, b * 64 + 64)
                        last = nc.vector.tensor_tensor(
                            on[r, :].rearrange("r (j p c) -> r j p c", p=2, c=DH),
                            y[r, :, 2 * DH * b:2 * DH * (b + 1)].rearrange("r j (p c) -> r j p c", p=2),
                            rden[r, :, :].unsqueeze(3).broadcast_to([64, J, 2, DH]), ALU.mult)
                    last.then_inc(s_norm, 1)

                def residual(t, u, par, stored):
                    dve.wait_ge(s_y, t + 1)
                    dve.wait_ge(s_xres, t + 1)
                    if stored is not None:
                        dve.wait_ge(s_x1st[par][u], stored)
                    nc.vector.tensor_tensor(x1[:, par, u, :], YB[:, P:2 * P], x_res[:, u, :], ALU.add).then_inc(s_res, 1)

                def ln2_stats(r, par):
                    dve.wait_ge(s_res, 4 * r + 4)
                    for u in range(U):
                        last = nc.vector.bn_stats(stat2[:, u, :], x1[:, par, u, :])
                    last.then_inc(s_st2, 1)

                def ln2_variance():
                    for u in range(U):
                        last = nc.vector.bn_aggr(mv2[:, u, :], stat2[:, u, :])
                    last.then_inc(s_mv2, 1)

                def wide(v):
                    return v[:, :].unsqueeze(2).broadcast_to([P, U, E])

                def take_logits(r):
                    dve.wait_ge(s_rl, r + 1)
                    if runs(r, 1):
                        dve.wait_ge(s_rex, r)
                    nc.vector.tensor_copy(lg[:, :, :], YB[:, 256:256 + U * E].rearrange("p (u e) -> p u e", e=E)
                                          ).then_inc(s_lg, 1)
                    dve.wait_ge(s_lg, r + 1)
                    nc.vector.reduce_max(r_max[:, :], lg[:, :, :], AX).then_inc(s_ch, 1)
                    dve.wait_ge(s_ch, r * CH + 1)
                    nc.vector.tensor_tensor(lg[:, :, :], lg[:, :, :], wide(r_max), ALU.subtract).then_inc(s_lsh, 1)

                def gate_probs(r):
                    def link(n, ins):
                        ins.then_inc(s_ch, 1)
                        dve.wait_ge(s_ch, r * CH + n)

                    dve.wait_ge(s_rex, r + 1)
                    link(2, nc.vector.reduce_sum(r_sum[:, :], ex[:, :, :], AX))
                    link(3, nc.vector.reciprocal(r_inv[:, :], r_sum[:, :]))
                    link(4, nc.vector.tensor_tensor(probs[:, :, :], ex[:, :, :], wide(r_inv), ALU.mult))

                def find_two_largest(r):
                    for u in range(U):
                        nc.vector.max(largest[:, u, :], probs[:, u, :]).then_inc(s_ch, 1)
                    dve.wait_ge(s_ch, r * CH + 8)
                    nc.vector.tensor_copy(two_largest[:, :, 0:KTOP], largest[:, :, 0:KTOP]).then_inc(s_ch, 1)

                def select(r):
                    for u in range(U):
                        last = nc.vector.match_replace(left[:, u, :], two_largest[:, u, :], probs[:, u, :], -1.0)
                    last.then_inc(s_left, 1)
                    dve.wait_ge(s_left, r + 1)
                    nc.vector.tensor_tensor(sel16[:, :, :], left[:, :, :], probs[:, :, :], ALU.not_equal
                                            ).then_inc(s_sel, 1)
                    dve.wait_ge(s_sel, r + 1)

                def write_gates(r, ir, par):
                    if runs(r, 2):
                        dve.wait_ge(s_scat[par], 16 * KTOP * U * ir)
                    nc.vector.tensor_tensor(rows[:, par, :, RGATE:RGATE + E], sel16[:, :, :], probs[:, :, :], ALU.mult
                                            ).then_inc(s_gate, 1)

                def positions(r, ir, par):
                    dve.wait_ge(s_rank, r + 1)
                    nc.vector.tensor_tensor(rank[:, :, :], YB[:, 288:288 + U * E].rearrange("p (u e) -> p u e", e=E),
                                            run_s[:, :].unsqueeze(1).broadcast_to([P, U, E]), ALU.add
                                            ).then_inc(s_pch, 1)
                    dve.wait_ge(s_pch, 6 * r + 1)
                    nc.vector.tensor_tensor(run_s[:, :], YB[:, 288 + U * E:288 + (U + 1) * E], run_s[:, :], ALU.add
                                            ).then_inc(s_pch, 1)
                    nc.vector.tensor_tensor(rank[:, :, :], rank[:, :, :], sel16[:, :, :], ALU.mult).then_inc(s_pch, 1)
                    dve.wait_ge(s_pch, 6 * r + 3)
                    nc.vector.reduce_max(pos_f[:, 0, :], rank[:, :, :], AX).then_inc(s_pch, 1)
                    nc.vector.reduce_sum(pos_f[:, 1, :], rank[:, :, :], AX).then_inc(s_pch, 1)
                    dve.wait_ge(s_pch, 6 * r + 5)
                    nc.vector.tensor_copy(pos[:, par, 0, :], pos_f[:, 0, :]).then_inc(s_pch, 1)
                    nc.vector.tensor_tensor(pos[:, par, 1, :], pos_f[:, 1, :], pos_f[:, 0, :], ALU.subtract
                                            ).then_inc(s_pos, 1)

                nc.vector.memset(q2[:, :, :, :, :], 0.0).then_inc(s_zero, 1)
                nc.vector.memset(ones16[:, :], 1.0).then_inc(s_zero, 1)
                nc.vector.memset(rows[:, :, :, :], 0.0).then_inc(s_zero, 1)
                nc.vector.memset(two_largest[:, :, :], -2.0).then_inc(s_two, 1)
                dve.wait_ge(s_w, 16 * NW)
                for u in range(U):
                    last = nc.vector.tensor_copy(vx[:, u, :, :], ones_s[:, :].unsqueeze(1).broadcast_to([P, J, VM]))
                last.then_inc(s_zero, 1)
                nc.vector.tensor_copy(bvb_s[:, :], bv_s[:, 0:1].broadcast_to([P, P])).then_inc(s_bvb, 1)
                dve.wait_ge(s_cv_ps, 1)
                nc.vector.tensor_tensor(cvec[:, :], YB[:, 0:D], bo_s[:, :], ALU.add).then_inc(s_cvec, 1)
                ln1_stats(0)
                dve.wait_ge(s_st1, 1)
                ln1_variance()
                make_mask(0)
                x_evac(0)
                ln1_stats(1)
                dve.wait_ge(s_st1, 2)
                dve.wait_ge(s_r1, 1)
                ln1_variance()
                dve.wait_ge(s_two, 1)
                dve.wait_ge(s_neg, 1)
                mask_scores(0, 0)
                shift_scores(0, 0)

                def body(s, i, par):
                    for u in range(U):
                        t = s * U + u
                        before = u or runs(s, 1)
                        after = u < U - 1 or runs(s, 0, NS - 2)
                        ahead = runs(s, 0, NS - 3)
                        if after:
                            if u or runs(s, 1):
                                dve.wait_ge(s_pt, 2 * t)
                            if u == U - 1:
                                dve.wait_ge(s_neg, s + 2)
                            if u == 1 and ahead:
                                dve.wait_ge(s_st1, s + 3)
                                dve.wait_ge(s_r1, s + 2)
                            if u == 2 and runs(s, 1):
                                dve.wait_ge(s_st2, s)
                                if runs(s, 2):
                                    dve.wait_ge(s_r2, s - 1)
                            mask_scores(t + 1, (u + 1) % U)
                        if u == 1 and ahead:
                            ln1_variance()
                        if u == 2 and runs(s, 1):
                            ln2_variance()
                        if before:
                            if u == 3 and runs(s, 2):
                                dve.wait_ge(s_ch, (s - 2) * CH + 9)
                            normalise(t - 1)
                        if u == 3 and runs(s, 2):
                            select(s - 2)
                            write_gates(s - 2, i - 1, par)
                        if after:
                            shift_scores(t + 1, (u + 1) % U)
                        if u == 0 and runs(s, 0, NS - 2):
                            x_evac(s + 1)
                        if u == 0 and ahead:
                            ln1_stats(s + 2)
                        if u == 1 and runs(s, 1):
                            ln2_stats(s - 1, 1 - par)
                        if u == 2 and runs(s, 2):
                            gate_probs(s - 2)
                        if u == 2 and runs(s, 0, NS - 2):
                            make_mask(s + 1)
                        if u == 2 and runs(s, 2):
                            find_two_largest(s - 2)
                        if before:
                            ppar, pi = (par, i) if u else (1 - par, i - 1 + par)
                            if u == 1 and runs(s, 2):
                                dve.wait_ge(s_xn2, s - 1)
                            residual(t - 1, (u - 1) % U, ppar, 16 * pi if runs(s, 2 if u else 3) else None)
                        if u == 1 and runs(s, 2):
                            take_logits(s - 2)
                        if u == 3 and runs(s, 2):
                            positions(s - 2, i - 1, par)

                for s in range(4):
                    body(s, s // 2, s % 2)
                with dve.Fori(2, NS // 2 - 2) as i:
                    for par in range(2):
                        body(2 * i + par, i, par)
                for s in range(NS - 4, NS):
                    body(s, s // 2, s % 2)
                normalise(NT - 1)
                residual(NT - 1, U - 1, 1, 16 * (NS // 2 - 1))
                ln2_stats(NS - 1, 1)
                dve.wait_ge(s_st2, NS)
                dve.wait_ge(s_r2, NS - 1)
                ln2_variance()
                take_logits(NS - 2)
                gate_probs(NS - 2)
                find_two_largest(NS - 2)
                dve.wait_ge(s_ch, (NS - 2) * CH + 9)
                select(NS - 2)
                write_gates(NS - 2, NS // 2 - 1, 0)
                positions(NS - 2, NS // 2 - 1, 0)
                take_logits(NS - 1)
                gate_probs(NS - 1)
                find_two_largest(NS - 1)
                dve.wait_ge(s_ch, (NS - 1) * CH + 9)
                select(NS - 1)
                write_gates(NS - 1, NS // 2 - 1, 1)
                positions(NS - 1, NS // 2 - 1, 1)

                k = [0]

                def link(ins):
                    k[0] += 1
                    ins.then_inc(s_tab, 1)
                    dve.wait_ge(s_tab, k[0])

                def over_blocks(v):
                    return v[:, :].unsqueeze(1).broadcast_to([P, NB, E])

                def over_experts(v):
                    return v[:, :].unsqueeze(2).broadcast_to([P, NB, E])

                nc.vector.tensor_copy(tails[:, :], run_s[:, :]).then_inc(s_tails, 1)
                link(nc.vector.tensor_tensor(count[:, :], run_s[:, :], region_s[:, :], ALU.subtract))
                link(nc.vector.tensor_scalar(past[:, :, 0:E], blocks_s[:, :, :], float(BLK), None, ALU.mult))
                link(nc.vector.tensor_tensor(skipped[:, :, :], past[:, :, :], over_blocks(count), ALU.is_lt))
                link(nc.vector.reduce_sum(blocks_of[:, :], skipped[:, :, :].rearrange("p b e -> p e b"), AX))
                link(nc.vector.tensor_copy(ends[:, :], blocks_of[:, :]))
                for e in range(1, E):
                    link(nc.vector.tensor_tensor(ends[:, e:e + 1], ends[:, e:e + 1], ends[:, e - 1:e], ALU.add))
                link(nc.vector.tensor_tensor(past[:, :, :], over_blocks(ends), blocks_s[:, :, :], ALU.is_le))
                link(nc.vector.reduce_sum(of_block[:, :], past[:, :, :], AX))
                link(nc.vector.tensor_tensor(skipped[:, :, :], past[:, :, :], over_blocks(blocks_of), ALU.mult))
                link(nc.vector.reduce_sum(start_of[:, :], skipped[:, :, :], AX))
                link(nc.vector.tensor_tensor(start_of[:, :], blocks_s[:, :, 0], start_of[:, :], ALU.subtract))
                link(nc.vector.tensor_scalar(row_f[:, :], of_block[:, :], float(REG), None, ALU.mult))
                link(nc.vector.scalar_tensor_tensor(out=row_f[:, :], in0=start_of[:, :], scalar=float(BLK),
                                                    in1=row_f[:, :], op0=ALU.mult, op1=ALU.add))
                link(nc.vector.memset(same[:, :], 0.0))
                link(nc.vector.tensor_tensor(same[:, 1:NB], of_block[:, 1:NB], of_block[:, 0:NB - 1], ALU.is_equal))
                link(nc.vector.tensor_scalar(active[:, :], of_block[:, :], float(E), None, ALU.is_lt))
                link(nc.vector.tensor_tensor(row_f[:, :], row_f[:, :], count[:, 0:1].broadcast_to([P, NB]), ALU.subtract))
                link(nc.vector.tensor_tensor(row_f[:, :], row_f[:, :], active[:, :], ALU.mult))
                link(nc.vector.tensor_tensor(row_f[:, :], row_f[:, :], count[:, 0:1].broadcast_to([P, NB]), ALU.add))
                link(nc.vector.tensor_tensor(of_block[:, :], of_block[:, :], active[:, :], ALU.mult))
                link(nc.vector.tensor_tensor(same[:, :], same[:, :], active[:, :], ALU.mult))
                link(nc.vector.tensor_tensor(same[:, :], rounds_s[:, :], same[:, :], ALU.subtract))
                link(nc.vector.tensor_scalar(table[:, 2, :], same[:, :], float(16 * BT), None, ALU.mult))
                link(nc.vector.tensor_copy(table[:, 0, :], row_f[:, :]))
                link(nc.vector.tensor_copy(table[:, 1, :], of_block[:, :]))
                nc.vector.tensor_tensor(expert_oh[:, :, :], over_blocks(experts_s), over_experts(of_block),
                                        ALU.is_equal).then_inc(s_tabd, 1)
                dve.wait_ge(s_tabd, 1)

                def pick_gates(b, i, r):
                    dve.wait_ge(s_xb[r], 16 * i + 16)
                    if not (isinstance(b, int) and b < R3):
                        dve.wait_ge(s_yb, b)
                    nc.vector.tensor_tensor(gtmp[:, :, :], xb[:, r, :, RGATE:RGATE + E],
                                            expert_oh[:, bass.ds(b, 1), :].broadcast_to([P, BT, E]), ALU.mult
                                            ).then_inc(s_gm, 1)
                    dve.wait_ge(s_gm, b + 1)
                    nc.vector.reduce_sum(gate[:, r, :], gtmp[:, :, :], AX).then_inc(s_gt, 1)

                def gated(b, i, r):
                    dve.wait_ge(s_gt, b + 1)
                    if not (isinstance(b, int) and b < R3):
                        dve.wait_ge(s_add[r], 16 * BT * i)
                    dve.wait_ge(s_dn, b + 1)
                    nc.vector.tensor_tensor(yb[:, r, :, :],
                                            DBK[r][:, 0:BT * D].rearrange("p (u d) -> p u d", d=D),
                                            gate[:, r, :].unsqueeze(2).broadcast_to([P, BT, D]), ALU.mult
                                            ).then_inc(s_yb, 1)

                for b in range(R3):
                    pick_gates(b, 0, b)
                    gated(b, 0, b)
                with dve.Fori(1, NB // R3) as i:
                    for r in range(R3):
                        pick_gates(R3 * i + r, i, r)
                        gated(R3 * i + r, i, r)


            @block.gpsimd
            def _(pool):
                def add_positions(s):
                    pool.wait_ge(s_ck, 16 * (s + 1))
                    v = ctx_k[:, :].rearrange("p (b k) -> p b k", k=L)
                    nc.gpsimd.tensor_tensor(v, v, pe_s[:, :].unsqueeze(1).broadcast_to([P, 2 * U, L]),
                                            ALU.add).then_inc(s_cp, 1)

                def rstd_1(s):
                    pool.wait_ge(s_stat, s + 1)
                    if runs(s, 1):
                        pool.wait_ge(s_xn, s)
                    nc.gpsimd.tensor_tensor(var1[:, :], mv1[:, :, 1], eps_s[:, :], ALU.add).then_inc(s_va1, 1)
                    nc.gpsimd.tensor_tensor(shift1[:, :], mv1[:, :, 0], minus_one[:, :], ALU.mult).then_inc(s_va1, 1)
                    pool.wait_ge(s_va1, 3 * s + 2)
                    nc.gpsimd.tensor_tensor(rstd1[:, :], var1[:, :], minus_half[:, :], ALU.pow).then_inc(s_va1, 1)
                    pool.wait_ge(s_va1, 3 * s + 3)
                    nc.gpsimd.tensor_tensor(shift1[:, :], shift1[:, :], rstd1[:, :], ALU.mult).then_inc(s_r1, 1)

                def spread_keys(t, u, par, reused=True):
                    if reused:
                        pool.wait_ge(s_sc, 2 * (t - 4) + 2)
                    for half in range(2):
                        last = nc.gpsimd.tensor_tensor(
                            kx[:, u, half, :, :], k2[:, par, half, u, :].unsqueeze(1).broadcast_to([P, HH, L]),
                            headmask[:, :].unsqueeze(2).broadcast_to([P, HH, L]), ALU.mult)
                    last.then_inc(s_kx, 1)

                def residual_bias(s, u):
                    pool.wait_ge(s_xr[u], 16 * (s + 1))
                    nc.gpsimd.tensor_tensor(x_res[:, u, :], x_res[:, u, :], cvec[:, :], ALU.add).then_inc(s_xres, 1)

                nc.gpsimd.memset(minus_half[:, :], -0.5).then_inc(s_mh, 1)
                nc.gpsimd.memset(eps_s[:, :], EPS).then_inc(s_mh, 1)
                nc.gpsimd.memset(minus_one[:, :], -1.0).then_inc(s_mh, 1)
                nc.gpsimd.memset(step_u[:, :], U * P).then_inc(s_mh, 1)
                nc.gpsimd.memset(zero_u[:, :], 0).then_inc(s_mh, 1)
                pool.wait_ge(s_mh, 5)
                pool.wait_ge(s_w, 16 * NW)
                add_positions(0)
                rstd_1(0)
                pool.wait_ge(s_kev, 1)
                spread_keys(0, 0, 0, False)
                add_positions(1)
                rstd_1(1)
                spread_keys(1, 1, 0, False)
                spread_keys(2, 2, 0, False)
                add_positions(2)
                pool.wait_ge(s_cvec, 1)

                def rstd_2(r):
                    pool.wait_ge(s_mv2, r + 1)
                    if runs(r, 1):
                        pool.wait_ge(s_xn2, r)
                    nc.gpsimd.tensor_tensor(var2[:, :], mv2[:, :, 1], eps_s[:, :], ALU.add).then_inc(s_va2, 1)
                    nc.gpsimd.tensor_tensor(shift2[:, :], mv2[:, :, 0], minus_one[:, :], ALU.mult).then_inc(s_va2, 1)
                    pool.wait_ge(s_va2, 3 * r + 2)
                    nc.gpsimd.tensor_tensor(rstd2[:, :], var2[:, :], minus_half[:, :], ALU.pow).then_inc(s_va2, 1)
                    pool.wait_ge(s_va2, 3 * r + 3)
                    nc.gpsimd.tensor_tensor(shift2[:, :], shift2[:, :], rstd2[:, :], ALU.mult).then_inc(s_r2, 1)

                def number_rows(r, par):
                    if runs(r, 1):
                        pool.wait_ge(s_tokadd, r)
                    pool.wait_ge(s_gate, r + 1)
                    pool.wait_ge(s_xn2, r + 1)
                    pool.wait_ge(s_pos, r + 1)
                    nc.gpsimd.tensor_tensor(rows[:, par, :, RTOK].bitcast(U32), tok_s[:, :], zero_u[:, :], ALU.add).then_inc(s_tok, 1)
                    pool.wait_ge(s_tok, r + 1)
                    nc.gpsimd.tensor_tensor(tok_s[:, :], tok_s[:, :], step_u[:, :], ALU.add).then_inc(s_tokadd, 1)

                def scatter_rows(par, tiles):
                    for u in tiles:
                        for k in range(KTOP):
                            nc.gpsimd.indirect_dma_start(
                                out=rows_d, out_offset=bass.IndirectOffsetOnAxis(ap=pos[:, par, k, u:u + 1], axis=0),
                                in_=rows[:, par, u, :], in_offset=None).then_inc(s_scat[par], 16)

                def body(s, i, par):
                    for u in range(U):
                        residual_bias(s, u)
                        if u == 0:
                            spread_keys(4 * s + 3, 3, par, runs(s, 1))
                            if runs(s, 3):
                                number_rows(s - 3, 1 - par)
                                scatter_rows(1 - par, (0, 1))
                        elif runs(s, 0, NS - 2):
                            if u == 1:
                                pool.wait_ge(s_kev, s + 2)
                            spread_keys(4 * s + 3 + u, u - 1, 1 - par)
                        if u == 1:
                            if runs(s, 0, NS - 3):
                                rstd_1(s + 2)
                            if runs(s, 3):
                                scatter_rows(1 - par, (2,))
                        if u == 2:
                            if runs(s, 1):
                                rstd_2(s - 1)
                            if runs(s, 3):
                                scatter_rows(1 - par, (3,))
                        if u == 3 and runs(s, 0, NS - 4):
                            add_positions(s + 3)

                for s in range(4):
                    body(s, s // 2, s % 2)
                with pool.Fori(2, NS // 2 - 2) as i:
                    for par in range(2):
                        body(2 * i + par, i, par)
                for s in range(NS - 4, NS):
                    body(s, s // 2, s % 2)
                number_rows(NS - 3, 1)
                scatter_rows(1, range(U))
                rstd_2(NS - 1)
                number_rows(NS - 2, 0)
                scatter_rows(0, range(U))
                number_rows(NS - 1, 1)
                scatter_rows(1, range(U))
                for par in range(2):
                    pool.wait_ge(s_scat[par], 16 * KTOP * U * (NS // 2))

                def tokens_of(r, loads):
                    pool.wait_ge(s_xb[r], 16 * loads)
                    nc.gpsimd.tensor_tensor(token[:, r, :], xb[:, r, :, RTOK].bitcast(U32), zero_u[:, 0:BT], ALU.add
                                            ).then_inc(s_tk, 1)

                def add_block(b, i, r):
                    if isinstance(b, int) and (b < 2 * R3 or b == NB - 1):
                        if b:
                            pool.wait_ge(s_add[(r - 1) % R3], 16 * BT * ((b - 1) // R3 + 1))
                    else:
                        pool.wait_ge(s_add[(r - 2) % R3], 16 * BT * (i + 1 if r == 2 else i))
                        needed = nc.values_load(table[0:1, 2, bass.ds(b, 1)], engines=[mybir.EngineType.Pool],
                                                min_val=16 * BT, max_val=16 * BT * (NB // R3))
                        pool.wait_ge(s_add[(r - 1) % R3], needed)
                    pool.wait_ge(s_yb, b + 1)
                    pool.wait_ge(s_tk, b + 1)
                    if not (isinstance(b, int) and b == NB - 1):
                        tokens_of((r + 1) % R3, i + 1 + (r + 1) // R3)
                    for u in range(BT):
                        nc.gpsimd.indirect_dma_start(
                            out=out, out_offset=bass.IndirectOffsetOnAxis(ap=token[:, r, u:u + 1], axis=0),
                            in_=yb[:, r, u, :], in_offset=None, compute_op=ALU.add).then_inc(s_add[r], 16)

                pool.wait_ge(s_tabd, 1)
                pool.wait_ge(s_init, 16)
                for par in range(2):
                    for u in range(U):
                        pool.wait_ge(s_x1st[par][u], 16 * (NS // 2))
                tokens_of(0, 1)
                for b in range(2 * R3):
                    add_block(b, b // R3, b % R3)
                with pool.Fori(2, NB // R3 - 1) as i:
                    for r in range(R3):
                        add_block(R3 * i + r, i, r)
                for r in range(R3):
                    add_block(NB - R3 + r, NB // R3 - 1, r)
                for r in range(R3):
                    pool.wait_ge(s_add[r], 16 * BT * (NB // R3))


def kernel(x, ctx_1024, mask_BxS2_bk0, L0_xattn_Wq, L0_xattn_bq, L0_xattn_Wk, L0_xattn_bk, L0_xattn_Wv, L0_xattn_bv,
           L0_xattn_Wo, L0_xattn_bo, L0_ffn_wg1, L0_ffn_bg1, L0_ffn_wg2, L0_ffn_w_in, L0_ffn_w_out):
    import concourse.bacc as bacc
    from concourse.bass_utils import run_bass_kernel_spmd

    def laid(a, *shape):
        a = np.asarray(a)
        return np.ascontiguousarray(a.reshape(shape) if shape else a)

    def turned(a):
        return np.ascontiguousarray(np.asarray(a).T)

    arrays = {
        "x": laid(x, N, D),
        "ctx_t": turned(laid(ctx_1024, N, D)),
        "mask": laid(mask_BxS2_bk0),
        "wq_t": turned(L0_xattn_Wq), "bq": laid(L0_xattn_bq),
        "wk_t": turned(L0_xattn_Wk), "bk": laid(L0_xattn_bk),
        "wv_t": turned(L0_xattn_Wv), "bv": laid(L0_xattn_bv),
        "wo_t": turned(L0_xattn_Wo), "bo": laid(L0_xattn_bo),
        "wg1": laid(L0_ffn_wg1), "bg1": laid(L0_ffn_bg1), "wg2": laid(L0_ffn_wg2),
        "w_in": laid(L0_ffn_w_in), "w_out": laid(L0_ffn_w_out),
    }
    nc = bacc.Bacc("TRN2", target_bir_lowering=False, num_devices=1)
    ins = [nc.dram_tensor(n, a.shape, mybir.dt.from_np(a.dtype), kind="ExternalInput").ap() for n, a in arrays.items()]
    out = nc.dram_tensor("out", [N + BLK, D], F32, kind="ExternalOutput").ap()
    build(nc, *ins, out)
    r = run_bass_kernel_spmd(nc, [arrays], core_ids=[0])
    return r.results[0]["out"][:N].reshape(B, L, D)
```

```python
from contextlib import ExitStack

import numpy as np

import concourse.bass as bass
from concourse import mybir

F32 = mybir.dt.float32
F16 = mybir.dt.float16
U8 = mybir.dt.uint8
U32 = mybir.dt.uint32
ALU = mybir.AluOpType
ACT = mybir.ActivationFunctionType
AX = mybir.AxisListType.X

P = 128
B, L, D = 128, 64, 128
H = 16
DH = D // H
HH = H // 2
E, HID, G = 8, 256, 32
N = B * L
NT = N // P
U = 4
NS = NT // U
SCALE = float(DH) ** -0.5
NEG = 10000000.0
NEG_A, NEG_B = 4000.0, 2500.0
assert NEG_A * NEG_B == NEG
EPS = 1e-5
VM = 64
J = H // 2
KTOP = 2
TABLE_LINKS = 14
BT = 4
BLK = BT * P
REG = N + BLK
R3 = 3
NB = -(-((KTOP * N + E * (BLK - 1)) // BLK) // R3) * R3
RW = 140
RTOK, RGATE = D, D + 4
CH = 9
PCH = 6


def position_encodings():
    half = D // 2
    periods = np.float32(1.0) / np.float32(10000.0) ** (np.arange(half, dtype=np.float32) / np.float32(half))
    angles = np.arange(L, dtype=np.float32)[:, None] * periods[None, :].astype(np.float32)
    return np.stack([np.sin(angles), np.cos(angles)], axis=-1).reshape(L, D).astype(np.float32)


def build(nc, x, ctxT, mask, wqT, bq, wkT, bk, wvT, bv, woT, bo, wg1, bg1, wg2, w_in, w_out, out):
    pe_c = nc.inline_tensor(np.ascontiguousarray(position_encodings().T), name="pe_t")
    ident_c = nc.inline_tensor(np.eye(P, dtype=np.float32), name="ident")
    head_of_row = (np.arange(P) % (D // 2)) // DH
    headmask_c = nc.inline_tensor((head_of_row[:, None] == np.arange(HH)[None, :]).astype(np.float32), name="headmask")
    q_of_row = np.arange(P) % L
    causal_c = nc.inline_tensor(
        np.where(np.arange(L)[None, :] > q_of_row[:, None], -NEG_A, 0.0).astype(np.float32), name="causal")
    spread_c = nc.inline_tensor((NEG_B * np.eye(P)).astype(np.float16), name="mask_spread")
    ones_cols = np.zeros((P, VM), np.float32)
    for p in range(2):
        ones_cols[p * L:(p + 1) * L, 4 * DH + p] = 1.0
    ones_c = nc.inline_tensor(ones_cols, name="value_ones")
    tri_c = nc.inline_tensor((np.arange(P)[:, None] < np.arange(P)[None, :]).astype(np.float16), name="before")
    region_c = nc.inline_tensor(np.tile(np.arange(E, dtype=np.float32) * REG, (P, 1)), name="region")
    tok_c = nc.inline_tensor(
        (np.arange(U)[None, :] * P + np.arange(P)[:, None]).astype(np.uint32), name="token")
    blocks_c = nc.inline_tensor(np.tile(np.repeat(np.arange(NB, dtype=np.float32), E), (P, 1)), name="block_numbers")
    block_rows_c = nc.inline_tensor(
        np.tile(np.repeat(np.arange(NB, dtype=np.float32) * BLK, E), (P, 1)), name="block_rows")
    up_to_c = nc.inline_tensor(np.tile(np.tril(np.ones((E, E), np.float32)).reshape(-1), (P, 1)), name="experts_up_to")
    rounds_c = nc.inline_tensor(
        np.tile((np.arange(NB) - 1) // R3 + 1, (P, 1)).astype(np.float32), name="rounds_before")
    experts_c = nc.inline_tensor(np.tile(np.arange(E, dtype=np.float32), (P, 1)), name="expert_numbers")
    pad_c = np.zeros((BLK, RW), np.float32)
    pad_c[:, RTOK] = (N + np.arange(BLK)).astype(np.uint32).view(np.float32)
    pad_c = nc.inline_tensor(pad_c, name="padding_rows")

    rows_d = nc.dram_tensor("routed_rows", [E * REG, RW], F32, kind="Internal").ap()

    x_r = x.rearrange("(t p) d -> p t d", p=P)
    out_r = out[0:N, :].rearrange("(t p) d -> p t d", p=P)

    with ExitStack() as ctx:
        def sb(name, shape, dt=F32):
            return ctx.enter_context(nc.sbuf_tensor(name, shape, dt))

        def sem(name):
            return ctx.enter_context(nc.semaphore(name))

        bank = [ctx.enter_context(nc.psum_tensor(f"bank{i}", [P, 512], F32)) for i in range(8)]
        W0, W1, SA, SB, PTA, PTB, XB, YB = bank
        PT_bank = [PTA, PTB]
        LOGITS, RANKS, COUNTS = 2 * P, 2 * P + U * E, 2 * P + 2 * U * E

        wq_s, wk_s, wv_s, wo_s = (sb(n, [P, D]) for n in ("wq_s", "wk_s", "wv_s", "wo_s"))
        bq_s, bk_s = sb("bq_s", [P, 1]), sb("bk_s", [P, 1])
        bq_scaled = sb("bq_scaled", [P, 1])
        bv_s, bo_s = sb("bv_s", [P, 1]), sb("bo_s", [P, D])
        bvb_s, cvec = sb("bvb_s", [P, P]), sb("cvec", [P, D])
        pe_s, ident = sb("pe_s", [P, L]), sb("ident_s", [P, P])
        headmask, causal = sb("headmask_s", [P, HH]), sb("causal_s", [P, L])
        ones_s = sb("ones_s", [P, VM])
        wg1_s, bg1_s, wg2_s = sb("wg1_s", [D, G]), sb("bg1_s", [G, 1]), sb("wg2_s", [G, E])
        tri_s, ones16 = sb("tri_s", [P, P], F16), sb("ones16", [P, P], F16)
        run_s, tok_s = sb("run_s", [P, E]), sb("tok_s", [P, U], U32)
        region_s = sb("region_s", [P, E])
        blocks_s, experts_s = sb("blocks_s", [P, NB, E]), sb("experts_s", [P, E])
        rounds_s = sb("rounds_s", [P, NB])
        block_rows, up_to = sb("block_rows_s", [P, NB, E]), sb("up_to_s", [P, E, E])
        pad_s = sb("pad_s", [P, BT, RW])

        x_in = sb("x_in", [P, U, D])
        ctx_k = sb("ctx_k", [P, U * P])
        ctx_v = sb("ctx_v", [P, U * P])
        mask_in = sb("mask_in", [P, U, L], U8)
        negmask = sb("negmask", [P, 2, U, L], F16)
        spread_s = sb("spread_s", [P, P], F16)
        x_res = sb("x_res", [P, U, D])
        stat1, mv1, rstd1 = sb("stat1", [P, U, 6]), sb("mv1", [P, U, 2]), sb("rstd1", [P, U])
        xn = sb("xn", [P, U, D])
        minus_half, eps_s = sb("minus_half", [P, U]), sb("eps_s", [P, U])
        step_u, zero_u = sb("step_u", [P, U], U32), sb("zero_u", [P, U], U32)
        minus_one = sb("minus_one", [P, U])
        var1, shift1 = sb("var1", [P, U]), sb("shift1", [P, U])
        xT = sb("xT", [P, U * P])
        q2 = sb("q2", [P, 2, 2, U, P])
        k2 = sb("k2", [P, 2, 2, U, L])
        kx = sb("kx", [P, U, 2, HH, L])
        vx = sb("vx", [P, U, J, VM])
        sm = sb("sm", [P, 2, H, L])
        smax = sb("smax", [P, H])
        pt = sb("pt", [P, J, P])
        xo = sb("xo", [P, 4, P])
        rden = sb("rden", [P, J, 2])
        on = sb("on", [P, D])
        onT = sb("onT", [P, P])
        x1 = sb("x1", [P, 2, U, D])

        stat2, mv2 = sb("stat2", [P, U, 6]), sb("mv2", [P, U, 2])
        var2, rstd2, shift2 = sb("var2", [P, U]), sb("rstd2", [P, U]), sb("shift2", [P, U])
        rows = sb("rows", [P, 3, U, RW])
        xt2 = sb("xt2", [P, U * P])
        hid_s = sb("hid_s", [G, U * P])
        lg, ex, probs, left = (sb(n, [P, U, E]) for n in ("lg", "ex", "probs", "left"))
        largest, two_largest = sb("largest", [P, U, 8]), sb("two_largest", [P, U, 8])
        r_max, r_sum, r_inv = (sb(n, [P, U]) for n in ("r_max", "r_sum", "r_inv"))
        sel16 = sb("sel16", [P, U, E], F16)
        rank = sb("rank", [P, U, E])
        pos_f = sb("pos_f", [P, KTOP, U])
        pos = sb("pos", [P, 3, KTOP, U], U32)
        (s_st2, s_mv2, s_va2, s_r2, s_xn2, s_rt, s_rte, s_rg, s_rge, s_rl, s_lg, s_lsh, s_rex, s_ch, s_sel, s_rank,
         s_pos, s_tokadd, s_tok, s_gate, s_pch, s_left, s_two) = (sem(n) for n in (
             "ln2_bn", "ln2_stats", "ln2_chain", "ln2_rstd", "rows_normed", "xn2_transposed", "xt2_ready",
             "hidden_in_psum", "hidden_ready", "logits_in_psum", "logits_copied", "logits_shifted", "logits_exp",
             "routing_chain", "selection_ready", "rank_in_psum", "positions_ready", "token_counted", "token_written",
             "gates_written", "positions_chain", "two_largest_replaced", "two_largest_filled"))
        s_scat = [sem(f"rows_scattered{i}") for i in range(2)]

        s_w, s_x, s_ck, s_cv, s_m = (sem(n) for n in (
            "projection_constants_in", "x_loaded", "ctx_k_loaded", "ctx_v_loaded", "mask_loaded"))
        s_xr = [sem(f"x_res_loaded{u}") for u in range(U)]
        s_x1st = [[sem(f"x1_stored{i}{u}") for u in range(U)] for i in range(2)]
        (s_zero, s_stat, s_xn, s_cp, s_neg, s_xt, s_xTs, s_k, s_kev, s_q, s_qev, s_v, s_vev, s_kx,
         s_sc, s_bqs, s_masked, s_max, s_sub, s_exp, s_pt, s_ptev, s_pv, s_xev, s_tq, s_rden, s_norm, s_ont,
         s_ontev, s_y, s_xres, s_res, s_bvb, s_cv_ps, s_cvec, s_r1, s_st1, s_va1, s_mh) = (sem(n) for n in (
             "zeroed", "ln1_stats", "xn_ready", "ctx_k_ready", "negmask_ready", "xT_in_psum", "xT_ready",
             "k_in_psum", "k2_ready", "q_in_psum", "q2_ready", "v_in_psum", "vx_ready", "kx_ready",
             "scores_in_psum", "bq_scaled", "scores_masked", "row_max", "scores_shifted", "probs_ready", "pt_in_psum",
             "pt_ready", "pv_in_psum", "xo_ready", "o_in_psum", "rden_ready", "o_normed", "onT_in_psum",
             "onT_ready", "y_in_psum", "x_res_ready", "x1_ready",
             "bv_spread", "cvec_in_psum", "cvec_ready", "ln1_rstd", "ln1_bn", "ln1_chain",
             "gpsimd_constants_set"))
        s_w2, s_w3 = sem("attention_constants_in"), sem("routing_constants_in")
        NW, NW2, NW3 = 6, 8, 12

        count = sb("count", [P, E])
        blocks_of, ends = sb("blocks_of", [P, E]), sb("ends", [P, E])
        past, skipped = sb("past", [P, NB, E]), sb("skipped", [P, NB, E])
        of_block = sb("of_block", [P, NB])
        start_of = sb("start_of", [P, NB])
        active, row_f = sb("active", [P, NB]), sb("row_f", [P, NB])
        same = sb("same", [P, NB])
        expert_oh = sb("expert_oh", [P, NB, E])
        table = sb("table", [P, 3, NB], U32)
        early_count = sb("early_count", [P, E])
        first_oh, had = sb("first_oh", [P, R3, E]), sb("had", [P, R3])
        sent = sb("sent", [P, 2, R3], U32)
        s_ofb, s_tabw, s_early = sem("experts_of_blocks"), sem("waits_ready"), sem("early_count_ready")
        tails = sb("tails", [P, E], U32)

        wi, wo = sb("wi", [P, R3, HID]), sb("wo", [P, E, 2, D])
        xb = sb("xb", [P, R3, BT, RW])
        xbT = sb("xbT", [P, R3, BLK])
        hb = sb("hb", [P, R3, 2, BLK])
        gtmp, gate = sb("gtmp", [P, BT, E]), sb("gate", [P, R3, BT])
        token = sb("token_ids", [P, R3, BT], U32)
        yb = sb("yb", [P, R3, BT, D])
        s_tab, s_tabd, s_tails, s_init, s_tail, s_wo = (sem(n) for n in (
            "table_chain", "table_ready", "tails_ready", "dummy_rows_zeroed", "padding_loaded_and_stored",
            "w_out_loaded"))
        s_xb = [sem(f"rows_loaded{i}") for i in range(R3)]
        s_wi = [sem(f"w_in_loaded{i}") for i in range(R3)]
        s_add = [sem(f"added_to_out{i}") for i in range(R3)]
        (s_bt, s_bte, s_up, s_gl, s_dn, s_gm, s_gt, s_tk, s_yb) = (sem(n) for n in (
            "block_transposed", "xbT_ready", "up_in_psum", "gelu_ready", "down_in_psum", "gate_masked", "gate_picked",
            "token_copied", "yb_ready"))
        TBK, UBK, DBK = bank[0:3], bank[3:5], bank[5:8]

        def runs(s, lo=0, hi=NS - 1):
            return not isinstance(s, int) or lo <= s <= hi

        with nc.Block() as block:
            @block.sync
            def _(sp):
                def load_x(s):
                    sp.dma_start(x_in[:, :, :], x_r[:, bass.ds(s * U, U), :]).then_inc(s_x, 16)

                def load_ctx_k(s):
                    sp.dma_start(ctx_k[:, :], ctxT[:, bass.ds(s * (U * P), U * P)]).then_inc(s_ck, 16)

                def load_ctx_v(s):
                    sp.dma_start(ctx_v[:, :], ctxT[:, bass.ds(s * (U * P), U * P)]).then_inc(s_cv, 16)

                def load_mask(s):
                    for b in range(2):
                        src = mask[bass.ds(s * (2 * U), 2 * U), :].rearrange("(u b) k -> b u k", b=2)[b]
                        sp.dma_start(mask_in[b * L:(b + 1) * L, :, :], src.partition_broadcast(L)).then_inc(s_m, 16)

                def load_x_res(s, u):
                    sp.dma_start(x_res[:, u, :], x_r[:, bass.ds(s * U + u, 1), :].rearrange("p a d -> p (a d)")
                                 ).then_inc(s_xr[u], 16)

                def store_tile(s, par, u):
                    t = s * U + u
                    sp.wait_ge(s_res, t + 1)
                    sp.dma_start(out_r[:, bass.ds(t, 1), :].rearrange("p a d -> p (a d)"), x1[:, par, u, :]
                                 ).then_inc(s_x1st[par][u], 16)

                load_ctx_k(0)
                load_x(0)
                load_mask(0)
                load_ctx_v(0)
                sp.dma_start(bv_s[:, :], bv.rearrange("(p a) -> p a", a=1)).then_inc(s_w2, 16)
                sp.dma_start(bo_s[:, :], bo.partition_broadcast(P)).then_inc(s_w2, 16)
                for u in range(U):
                    load_x_res(0, u)
                for dst, src in ((wg1_s[:, :], wg1), (bg1_s[:, :], bg1.rearrange("(p a) -> p a", a=1)),
                                 (wg2_s[:, :], wg2), (tri_s[:, :], tri_c.ap()), (run_s[:, :], region_c.ap()),
                                 (region_s[:, :], region_c.ap()), (tok_s[:, :], tok_c.ap()),
                                 (blocks_s[:, :, :].rearrange("p b e -> p (b e)"), blocks_c.ap()),
                                 (experts_s[:, :], experts_c.ap()), (rounds_s[:, :], rounds_c.ap()),
                                 (block_rows[:, :, :].rearrange("p b e -> p (b e)"), block_rows_c.ap()),
                                 (up_to[:, :, :].rearrange("p a b -> p (a b)"), up_to_c.ap())):
                    sp.dma_start(dst, src).then_inc(s_w3, 16)
                sp.dma_start(pad_s[:, :, :], pad_c.ap().rearrange("(u p) w -> p u w", p=P)).then_inc(s_tail, 16)
                sp.wait_ge(s_xn, 1)
                load_x(1)
                sp.wait_ge(s_k, 1)
                load_ctx_k(1)
                sp.wait_ge(s_v, 1)
                load_ctx_v(1)
                sp.wait_ge(s_neg, 1)
                load_mask(1)
                sp.wait_ge(s_xn, 2)
                load_x(2)
                sp.wait_ge(s_k, 2)
                load_ctx_k(2)
                sp.dma_start(wo[:, :, :, :].rearrange("p e c d -> p (e c) d"),
                             w_out.rearrange("e (c p) d -> p (e c) d", p=P)).then_inc(s_wo, 16)
                sp.wait_ge(s_tail, 16)

                def body(s, par):
                    for u in range(U):
                        if u == 2 and runs(s, 0, NS - 3):
                            sp.wait_ge(s_neg, s + 2)
                            load_mask(s + 2)
                        if u == 3 and runs(s, 0, NS - 4):
                            sp.wait_ge(s_k, s + 3)
                            load_ctx_k(s + 3)
                            sp.wait_ge(s_xn, s + 3)
                            load_x(s + 3)
                        if u == 3 and runs(s, 0, NS - 3):
                            sp.wait_ge(s_v, s + 2)
                            load_ctx_v(s + 2)
                        if u > 1 or runs(s, 1):
                            ps, ppar, pu = (s, par, u - 2) if u > 1 else (s - 1, 1 - par, u + 2)
                            store_tile(ps, ppar, pu)
                            if u < 2 or runs(s, 0, NS - 2):
                                load_x_res(ps + 1, pu)

                for s in range(4):
                    body(s, s % 2)
                with sp.Fori(2, NS // 2 - 2) as i:
                    for par in range(2):
                        body(2 * i + par, par)
                for s in range(NS - 4, NS):
                    body(s, s % 2)
                for u in (U - 2, U - 1):
                    store_tile(NS - 1, 1, u)
                for par in range(2):
                    for u in range(U):
                        sp.wait_ge(s_x1st[par][u], 16 * (NS // 2))

                def pad_region(e):
                    at = nc.values_load(tails[0:1, e:e + 1], engines=[mybir.EngineType.SP], min_val=e * REG,
                                        max_val=e * REG + N)
                    sp.dma_start(rows_d[bass.ds(at, BLK), :].rearrange("(u p) w -> p u w", p=P), pad_s[:, :, :]
                                 ).then_inc(s_tail, 16)

                def load_block(b, r):
                    expert = nc.values_load(table[0:1, 1, bass.ds(b, 1)], engines=[mybir.EngineType.SP],
                                            min_val=0, max_val=E - 1)
                    at = nc.values_load(table[0:1, 0, bass.ds(b, 1)], engines=[mybir.EngineType.SP],
                                        min_val=0, max_val=E * REG - BLK)
                    if isinstance(b, int) and b < R3:
                        rows_sent = nc.values_load(sent[0:1, 0, b:b + 1], engines=[mybir.EngineType.SP],
                                                   min_val=16 * KTOP * U * (NS // 2 - 1),
                                                   max_val=16 * KTOP * U * (NS // 2))
                        padding_sent = nc.values_load(sent[0:1, 1, b:b + 1], engines=[mybir.EngineType.SP],
                                                      min_val=16, max_val=16 + 16 * E)
                        sp.dma_start(wi[:, r, :], w_in[bass.ds(expert, 1), :, :].rearrange("e d h -> d (e h)")
                                     ).then_inc(s_wi[r], 16)
                        sp.wait_ge(s_tail, padding_sent)
                        for par in range(2):
                            sp.wait_ge(s_scat[par], rows_sent)
                    else:
                        sp.wait_ge(s_bt, b - R3 + 1)
                        sp.wait_ge(s_tk, b - R3 + 1)
                        sp.wait_ge(s_gm, b - R3 + 1)
                    sp.dma_start(xb[:, r, :, :], rows_d[bass.ds(at, BLK), :].rearrange("(u p) w -> p u w", p=P)
                                 ).then_inc(s_xb[r], 16)
                    if not (isinstance(b, int) and b < R3):
                        sp.wait_ge(s_up, 2 * (b - R3 + 1))
                        sp.dma_start(wi[:, r, :], w_in[bass.ds(expert, 1), :, :].rearrange("e d h -> d (e h)")
                                     ).then_inc(s_wi[r], 16)

                sp.dma_start(out[N:N + BLK, :].rearrange("(u p) d -> p u d", p=P), pad_s[:, :, 0:D]).then_inc(s_init, 16)
                sp.wait_ge(s_tails, 1)
                for e in range(E // 2):
                    pad_region(e)
                sp.wait_ge(s_tabd, 2)
                sp.wait_ge(s_tab, TABLE_LINKS)
                for b in range(R3):
                    load_block(b, b)
                sp.wait_ge(s_tail, 16 + 16 * E)
                for par in range(2):
                    sp.wait_ge(s_scat[par], 16 * KTOP * U * (NS // 2))
                with sp.Fori(1, NB // R3) as i:
                    for r in range(R3):
                        load_block(R3 * i + r, r)

            @block.tensor
            def _(pe):
                def t_x(s):
                    pe.wait_ge(s_xn, s + 1)
                    for u in range(U):
                        last = nc.tensor.transpose(W0[:, u * P:(u + 1) * P], xn[:, u, :], ident[:, :])
                    last.then_inc(s_xt, 1)

                def project_k(s):
                    pe.wait_ge(s_cp, s + 1)
                    nc.tensor.matmul(W1[:, :], wk_s[:, :], ctx_k[:, :], start=True, stop=True).then_inc(s_k, 1)

                def project_q(s):
                    pe.wait_ge(s_xTs, s + 1)
                    nc.tensor.matmul(W0[:, :], wq_s[:, :], xT[:, :], start=True, stop=True).then_inc(s_q, 1)

                def project_v(s):
                    pe.wait_ge(s_cv, 16 * (s + 1))
                    pe.wait_ge(s_qev, s + 1)
                    for u in range(U):
                        last = nc.tensor.matmul(W0[:, u * P:(u + 1) * P], ctx_v[:, u * P:(u + 1) * P], wv_s[:, :],
                                                start=True, stop=True)
                    last.then_inc(s_v, 1)

                def scores(t, u, par, first=False):
                    pe.wait_ge(s_kx, t + 1)
                    if not first:
                        pe.wait_ge(s_sub, 2 * t - 1)
                    nc.tensor.matmul(SA[:, :], q2[:, par, 0, u, :], kx[:, u, 0, :, :].rearrange("p h k -> p (h k)"),
                                     start=True, stop=False)
                    nc.tensor.matmul(SA[:, :].rearrange("p (h k) -> p h k", k=L), spread_s[:, :],
                                     negmask[:, par, u, :].unsqueeze(1).broadcast_to([P, HH, L]),
                                     start=False, stop=True).then_inc(s_sc, 1)
                    if not first:
                        pe.wait_ge(s_masked, t)
                    nc.tensor.matmul(SB[:, :], q2[:, par, 1, u, :], kx[:, u, 1, :, :].rearrange("p h k -> p (h k)"),
                                     start=True, stop=True).then_inc(s_sc, 1)

                def transpose_probs(t, u):
                    pr = sm[:, u % 2, :, :].rearrange("p h k -> p (h k)")
                    for j in range(J):
                        if j % 4 == 0:
                            pe.wait_ge(s_exp, 2 * t + j // 4 + 1)
                        last = nc.tensor.transpose(PT_bank[j // 4][:, (j % 4) * P:(j % 4 + 1) * P],
                                                   pr[:, j * P:(j + 1) * P], ident[:, :])
                        if j % 4 == 3:
                            last.then_inc(s_pt, 1)

                def values(t, u):
                    pe.wait_ge(s_ptev, 2 * t + 2)
                    for j in range(J):
                        o = VM * (j % 2)
                        last = nc.tensor.matmul(XB[o:o + VM, (j // 2) * P:(j // 2 + 1) * P], vx[:, u, j, :],
                                                pt[:, j, :], start=True, stop=True)
                    last.then_inc(s_pv, 1)

                def queries_to_rows(t):
                    pe.wait_ge(s_xev, t + 1)
                    for c in range(4):
                        last = nc.tensor.transpose(YB[:, c * P:(c + 1) * P], xo[:, c, :], ident[:, :])
                    last.then_inc(s_tq, 1)

                def transpose_o(t):
                    pe.wait_ge(s_norm, t + 1)
                    nc.tensor.transpose(YB[:, 0:P], on[:, :], ident[:, :]).then_inc(s_ont, 1)

                def project_o(t):
                    pe.wait_ge(s_ontev, t + 1)
                    nc.tensor.matmul(YB[:, P:2 * P], onT[:, :], wo_s[:, :], start=True, stop=True).then_inc(s_y, 1)

                pe.wait_ge(s_w, 16 * NW)
                project_k(0)
                t_x(0)
                project_q(0)
                pe.wait_ge(s_w2, 16 * NW2)
                pe.wait_ge(s_bvb, 1)
                nc.tensor.matmul(YB[:, 0:D], bvb_s[:, :], wo_s[:, :], start=True, stop=True).then_inc(s_cv_ps, 1)
                pe.wait_ge(s_kev, 1)
                project_k(1)
                pe.wait_ge(s_qev, 1)
                pe.wait_ge(s_neg, 1)
                scores(0, 0, 0, True)
                project_v(0)
                scores(1, 1, 0)
                pe.wait_ge(s_cvec, 1)

                pe.wait_ge(s_w3, 16 * NW3)

                def transpose_rows(r, par):
                    pe.wait_ge(s_xn2, r + 1)
                    for u in range(U):
                        last = nc.tensor.transpose(W1[:, u * P:(u + 1) * P], rows[:, par, u, 0:D], ident[:, :])
                    last.then_inc(s_rt, 1)

                def gate_hidden(r):
                    pe.wait_ge(s_rte, r + 1)
                    nc.tensor.matmul(W1[0:G, :], wg1_s[:, :], xt2[:, :], start=True, stop=True).then_inc(s_rg, 1)

                def gate_logits(r):
                    pe.wait_ge(s_rge, r + 1)
                    for u in range(U):
                        last = nc.tensor.matmul(YB[:, LOGITS + u * E:LOGITS + (u + 1) * E], hid_s[:, u * P:(u + 1) * P],
                                                wg2_s[:, :], start=True, stop=True)
                    last.then_inc(s_rl, 1)

                def rank_tokens(r):
                    pe.wait_ge(s_sel, r + 1)
                    o, n = RANKS, COUNTS
                    nc.tensor.matmul(YB[:, o:n], tri_s[:, :], sel16[:, :, :].rearrange("p u e -> p (u e)"),
                                     start=True, stop=False, skip_group_check=True)
                    for k in range(1, U):
                        nc.tensor.matmul(YB[:, o + k * E:n], ones16[:, :],
                                         sel16[:, 0:U - k, :].rearrange("p u e -> p (u e)"),
                                         start=False, stop=False, skip_group_check=True)
                    for u in range(U):
                        last = nc.tensor.matmul(YB[:, n:n + E], ones16[:, :], sel16[:, u, :],
                                                start=False, stop=(u == U - 1), skip_group_check=True)
                    last.then_inc(s_rank, 1)

                def body(s, par):
                    for u in range(U):
                        t = s * U + u
                        before = u or runs(s, 1)
                        transpose_probs(t, u)
                        if before:
                            if u > 1 or runs(s, 1):
                                pe.wait_ge(s_res, t - 1)
                            if u == 2 and runs(s, 2):
                                pe.wait_ge(s_lg, s - 1)
                            if u == 0 and runs(s, 3):
                                pe.wait_ge(s_pch, PCH * (s - 3) + 2)
                            queries_to_rows(t - 1)
                        if u == 0 and runs(s, 0, NS - 2):
                            pe.wait_ge(s_vev, s + 1)
                            t_x(s + 1)
                        if u == 1 and runs(s, 0, NS - 2):
                            project_q(s + 1)
                        if u == 2 and runs(s, 0, NS - 3):
                            pe.wait_ge(s_kev, s + 2)
                            if runs(s, 2):
                                pe.wait_ge(s_rge, s - 1)
                            project_k(s + 2)
                        if u < 2 or runs(s, 0, NS - 2):
                            if u == 2:
                                pe.wait_ge(s_qev, s + 2)
                                pe.wait_ge(s_neg, s + 2)
                            scores(t + 2, (u + 2) % U, par if u < 2 else 1 - par)
                        if u == 0 and runs(s, 2):
                            if runs(s, 0, NS - 2):
                                pe.wait_ge(s_kev, s + 2)
                            transpose_rows(s - 2, par)
                        if before:
                            transpose_o(t - 1)
                        if u == 3 and runs(s, 0, NS - 2):
                            project_v(s + 1)
                        if u == 0:
                            pe.wait_ge(s_vev, s + 1)
                        values(t, u)
                        if before:
                            pe.wait_ge(s_ontev, t)
                            if u == 1 and runs(s, 2):
                                gate_logits(s - 2)
                            if u == 3 and runs(s, 2):
                                rank_tokens(s - 2)
                            project_o(t - 1)
                        if u == 0 and runs(s, 2):
                            gate_hidden(s - 2)

                for s in range(4):
                    body(s, s % 2)
                with pe.Fori(2, NS // 2 - 2) as i:
                    for par in range(2):
                        body(2 * i + par, par)
                for s in range(NS - 4, NS):
                    body(s, s % 2)
                pe.wait_ge(s_res, NT - 1)
                pe.wait_ge(s_pos, NS - 2)
                queries_to_rows(NT - 1)
                transpose_rows(NS - 2, 0)
                transpose_o(NT - 1)
                gate_hidden(NS - 2)
                pe.wait_ge(s_ontev, NT)
                project_o(NT - 1)
                pe.wait_ge(s_res, NT)
                gate_logits(NS - 2)
                pe.wait_ge(s_rge, NS - 1)
                transpose_rows(NS - 1, 2)
                pe.wait_ge(s_lg, NS - 1)
                rank_tokens(NS - 2)
                gate_hidden(NS - 1)
                pe.wait_ge(s_pos, NS - 1)
                gate_logits(NS - 1)
                pe.wait_ge(s_lg, NS)
                rank_tokens(NS - 1)

                def expert_of(b):
                    return nc.values_load(table[0:1, 1, bass.ds(b, 1)], engines=[mybir.EngineType.PE],
                                          min_val=0, max_val=E - 1)

                def transposes(b, i, r):
                    pe.wait_ge(s_xb[r], 16 * i + 16)
                    if not (isinstance(b, int) and b < R3):
                        pe.wait_ge(s_bte, b - R3 + 1)
                    for u in range(BT):
                        last = nc.tensor.transpose(TBK[r][:, u * P:(u + 1) * P], xb[:, r, u, 0:D], ident[:, :])
                    last.then_inc(s_bt, 1)

                def up(b, i, r, first=False):
                    pe.wait_ge(s_wi[r], 16 * i + 16)
                    pe.wait_ge(s_bte, b + 1)
                    if not first:
                        pe.wait_ge(s_gl, 2 * b)
                    for c in range(2):
                        nc.tensor.matmul(UBK[c][:, 0:BLK],
                                         wi[:, r, c * P:(c + 1) * P],
                                         xbT[:, r, :], start=True, stop=True).then_inc(s_up, 1)

                def down(b, r):
                    e = expert_of(b)
                    pe.wait_ge(s_gl, 2 * b + 2)
                    if not (isinstance(b, int) and b < R3):
                        pe.wait_ge(s_yb, b - R3 + 1)
                    for u in range(BT):
                        for c in range(2):
                            last = nc.tensor.matmul(DBK[r][:, u * D:(u + 1) * D], hb[:, r, c, u * P:(u + 1) * P],
                                                    wo[:, bass.ds(e, 1), c, :].rearrange("p e d -> p (e d)"),
                                                    start=(c == 0), stop=(c == 1))
                    last.then_inc(s_dn, 1)

                pe.wait_ge(s_wo, 16)
                pe.wait_ge(s_tabd, 1)
                transposes(0, 0, 0)
                up(0, 0, 0, True)
                transposes(1, 0, 1)
                down(0, 0)
                up(1, 0, 1)
                transposes(2, 0, 2)
                for b in range(1, R3):
                    up(b + 1, (b + 1) // R3, (b + 1) % R3)
                    transposes(b + 2, (b + 2) // R3, (b + 2) % R3)
                    down(b, b)
                with pe.Fori(1, NB // R3 - 1) as i:
                    for r in range(R3):
                        b = R3 * i + r
                        up(b + 1, i + (r + 1) // R3, (r + 1) % R3)
                        transposes(b + 2, i + (r + 2) // R3, (r + 2) % R3)
                        down(b, r)
                for r in range(R3):
                    b = NB - R3 + r
                    if r < R3 - 1:
                        up(b + 1, NB // R3 - 1, r + 1)
                    if r < R3 - 2:
                        transposes(b + 2, NB // R3 - 1, r + 2)
                    down(b, r)

            @block.scalar
            def _(act):
                def k_evac(s, par):
                    act.wait_ge(s_k, s + 1)
                    src = W1[:, :].rearrange("c (u b k) -> c u b k", u=U, b=2)
                    for half in range(2):
                        r = slice(half * 64, half * 64 + 64)
                        for b in range(2):
                            last = nc.scalar.activation(k2[b * 64:b * 64 + 64, par, half, :, :], src[r, :, b, :],
                                                        ACT.Identity, bias=bk_s[r, :])
                    last.then_inc(s_kev, 1)

                def q_evac(s, par):
                    act.wait_ge(s_q, s + 1)
                    src = W0[:, :].rearrange("c (u b k) -> c u b k", u=U, b=2)
                    for half in range(2):
                        r = slice(half * 64, half * 64 + 64)
                        for b in range(2):
                            last = nc.scalar.activation(q2[b * 64:b * 64 + 64, par, half, :, b * L:(b + 1) * L],
                                                        src[r, :, b, :], ACT.Identity, bias=bq_scaled[r, :],
                                                        scale=SCALE)
                    last.then_inc(s_qev, 1)

                def v_evac(s):
                    act.wait_ge(s_v, s + 1)
                    src = W0[:, :].rearrange("r (uj p c) -> r uj p c", p=2, c=DH)
                    dst = vx[:, :, :, :].rearrange("r u j m -> r (u j) m")
                    for b in range(2):
                        for p in range(2):
                            o = (2 * b + p) * DH
                            last = nc.scalar.activation(dst[p * 64:p * 64 + 64, :, o:o + DH],
                                                        src[b * 64:b * 64 + 64, :, p, :], ACT.Copy)
                    last.then_inc(s_vev, 1)

                def exps(t, u):
                    for half in range(2):
                        act.wait_ge(s_sub, 2 * t + half + 1)
                        heads = sm[:, u % 2, half * HH:(half + 1) * HH, :]
                        nc.scalar.activation(heads, heads, ACT.Exp).then_inc(s_exp, 1)

                def onT_evac(t):
                    act.wait_ge(s_ont, t + 1)
                    nc.scalar.activation(onT[:, :], YB[:, 0:P], ACT.Copy).then_inc(s_ontev, 1)

                for dst, src in ((pe_s[:, :], pe_c.ap()), (wk_s[:, :], wkT), (ident[:, :], ident_c.ap()), (wq_s[:, :], wqT),
                                 (bk_s[:, :], bk.rearrange("(p a) -> p a", a=1)),
                                 (bq_s[:, :], bq.rearrange("(p a) -> p a", a=1))):
                    act.dma_start(dst, src).then_inc(s_w, 16)
                for dst, src in ((spread_s[:, :], spread_c.ap()), (headmask[:, :], headmask_c.ap()),
                                 (causal[:, :], causal_c.ap()),
                                 (wv_s[:, :], wvT), (ones_s[:, :], ones_c.ap()), (wo_s[:, :], woT)):
                    act.dma_start(dst, src).then_inc(s_w2, 16)

                def ln1_norm(s):
                    act.wait_ge(s_r1, s + 1)
                    for u in range(U):
                        last = nc.scalar.activation(xn[:, u, :], x_in[:, u, :], ACT.Identity,
                                                    bias=shift1[:, u:u + 1], scale=rstd1[:, u:u + 1])
                    last.then_inc(s_xn, 1)

                def ln2_norm(r, ir, par):
                    if runs(r, 2) and par < 2:
                        act.wait_ge(s_scat[par], 16 * KTOP * U * ir)
                    act.wait_ge(s_r2, r + 1)
                    for u in range(U):
                        last = nc.scalar.activation(rows[:, par, u, 0:D], x1[:, min(par, 1), u, :], ACT.Identity,
                                                    bias=shift2[:, u:u + 1], scale=rstd2[:, u:u + 1])
                    last.then_inc(s_xn2, 1)

                ln1_norm(0)
                act.wait_ge(s_w, 16 * NW)
                k_evac(0, 0)
                act.wait_ge(s_bqs, 1)
                act.wait_ge(s_zero, 3)
                q_evac(0, 0)
                act.wait_ge(s_xt, 1)
                ln1_norm(1)
                k_evac(1, 1)
                act.wait_ge(s_zero, 4)
                v_evac(0)
                exps(0, 0)

                act.wait_ge(s_w3, 16 * NW3)

                def xt2_evac(r):
                    act.wait_ge(s_rt, r + 1)
                    nc.scalar.activation(xt2[:, :], W1[:, :], ACT.Copy).then_inc(s_rte, 1)

                def gate_gelu(r):
                    act.wait_ge(s_rg, r + 1)
                    if runs(r, 1):
                        act.wait_ge(s_rl, r)
                    nc.scalar.activation(hid_s[:, :], W1[0:G, :], ACT.Gelu, bias=bg1_s[:, :]).then_inc(s_rge, 1)

                def gate_exp(r):
                    act.wait_ge(s_lsh, r + 1)
                    nc.scalar.activation(ex[:, :, :], lg[:, :, :], ACT.Exp).then_inc(s_rex, 1)

                def body(s, i, par):
                    for u in range(U):
                        t = s * U + u
                        for c in range(2):
                            act.wait_ge(s_pt, 2 * t + c + 1)
                            nc.scalar.activation(pt[:, 4 * c:4 * c + 4, :].rearrange("p j q -> p (j q)"),
                                                 PT_bank[c][:, :], ACT.Copy).then_inc(s_ptev, 1)
                        if u < U - 1 or runs(s, 0, NS - 2):
                            exps(t + 1, u + 1)
                        if u == 0 and runs(s, 2):
                            xt2_evac(s - 2)
                        if u == 2 and runs(s, 2):
                            gate_exp(s - 2)
                        if u or runs(s, 1):
                            onT_evac(t - 1)
                        if u == 2 and runs(s, 0, NS - 3):
                            act.wait_ge(s_kx, 4 * s + 4)
                            k_evac(s + 2, par)
                        if u == 1 and runs(s, 0, NS - 2):
                            q_evac(s + 1, 1 - par)
                        act.wait_ge(s_pv, t + 1)
                        nc.scalar.activation(xo[:, :, :].rearrange("p c q -> p (c q)"), XB[:, :], ACT.Copy
                                             ).then_inc(s_xev, 1)
                        if u == 0 and runs(s, 2):
                            gate_gelu(s - 2)
                        if u == 2 and runs(s, 0, NS - 3):
                            act.wait_ge(s_xt, s + 2)
                            ln1_norm(s + 2)
                        if u == 3 and runs(s, 0, NS - 2):
                            v_evac(s + 1)
                        if u == 3 and runs(s, 1):
                            ln2_norm(s - 1, i - 1 + par, 1 - par)

                for s in range(4):
                    body(s, s // 2, s % 2)
                with act.Fori(2, NS // 2 - 2) as i:
                    for par in range(2):
                        body(2 * i + par, i, par)
                for s in range(NS - 4, NS):
                    body(s, s // 2, s % 2)
                xt2_evac(NS - 2)
                onT_evac(NT - 1)
                gate_gelu(NS - 2)
                gate_exp(NS - 2)
                ln2_norm(NS - 1, NS // 2 - 1, 2)
                xt2_evac(NS - 1)
                gate_gelu(NS - 1)
                gate_exp(NS - 1)

                def pad_region(e):
                    at = nc.values_load(tails[0:1, e:e + 1], engines=[mybir.EngineType.Activation], min_val=e * REG,
                                        max_val=e * REG + N)
                    act.dma_start(rows_d[bass.ds(at, BLK), :].rearrange("(u p) w -> p u w", p=P), pad_s[:, :, :]
                                  ).then_inc(s_tail, 16)

                def xbT_evac(b, r):
                    act.wait_ge(s_bt, b + 1)
                    if not (isinstance(b, int) and b < R3):
                        act.wait_ge(s_up, 2 * (b - R3 + 1))
                    nc.scalar.activation(xbT[:, r, :], TBK[r][:, 0:BLK], ACT.Copy).then_inc(s_bte, 1)

                def gelus(b, r):
                    for c in range(2):
                        act.wait_ge(s_up, 2 * b + c + 1)
                        if not (isinstance(b, int) and b < R3):
                            act.wait_ge(s_dn, b - R3 + 1)
                        nc.scalar.activation(hb[:, r, c, :], UBK[c][:, 0:BLK], ACT.Gelu).then_inc(s_gl, 1)

                act.wait_ge(s_tail, 16)
                act.wait_ge(s_tails, 1)
                for e in range(E // 2, E):
                    pad_region(e)
                xbT_evac(0, 0)
                gelus(0, 0)
                xbT_evac(1, 1)
                for b in range(R3):
                    gelus(b + 1, (b + 1) % R3)
                    xbT_evac(b + 2, (b + 2) % R3)
                with act.Fori(1, NB // R3 - 1) as i:
                    for r in range(R3):
                        gelus(R3 * i + r + 1, (r + 1) % R3)
                        xbT_evac(R3 * i + r + 2, (r + 2) % R3)
                for r in range(R3):
                    if r < R3 - 1:
                        gelus(NB - R3 + r + 1, r + 1)
                    if r < R3 - 2:
                        xbT_evac(NB - R3 + r + 2, r + 2)
            @block.vector
            def _(dve):
                def ln1_stats(s):
                    dve.wait_ge(s_x, 16 * (s + 1))
                    for u in range(U):
                        last = nc.vector.bn_stats(stat1[:, u, :], x_in[:, u, :])
                    last.then_inc(s_st1, 1)

                def ln1_variance():
                    for u in range(U):
                        last = nc.vector.bn_aggr(mv1[:, u, :], stat1[:, u, :])
                    last.then_inc(s_stat, 1)

                def x_evac(s):
                    dve.wait_ge(s_xt, s + 1)
                    nc.vector.tensor_tensor(xT[:, :].rearrange("p (b k) -> p b k", k=L),
                                            W0[:, :].rearrange("p (b k) -> p b k", k=L),
                                            pe_s[:, :].unsqueeze(1).broadcast_to([P, 2 * U, L]), ALU.add
                                            ).then_inc(s_xTs, 1)

                def make_mask(s, par):
                    dve.wait_ge(s_m, 32 * (s + 1))
                    nc.vector.scalar_tensor_tensor(out=negmask[:, par, :, :], in0=mask_in[:, :, :], scalar=-NEG_A,
                                                   in1=causal[:, :].unsqueeze(1).broadcast_to([P, U, L]),
                                                   op0=ALU.mult, op1=ALU.min).then_inc(s_neg, 1)

                def row_maxima(t, u, par):
                    dve.wait_ge(s_sc, 2 * t + 1)
                    nc.vector.reduce_max(smax[:, 0:HH], SA[:, :].rearrange("p (h k) -> p h k", k=L), AX
                                         ).then_inc(s_max, 1)
                    dve.wait_ge(s_sc, 2 * t + 2)
                    nc.vector.scalar_tensor_tensor(
                        out=sm[:, u % 2, HH:H, :], in0=negmask[:, par, u, :].unsqueeze(1).broadcast_to([P, HH, L]),
                        scalar=NEG_B, in1=SB[:, :].rearrange("p (h k) -> p h k", k=L), op0=ALU.mult, op1=ALU.add
                        ).then_inc(s_masked, 1)
                    dve.wait_ge(s_masked, t + 1)
                    nc.vector.reduce_max(smax[:, HH:H], sm[:, u % 2, HH:H, :], AX).then_inc(s_max, 1)

                def subtract_maxima(t, u):
                    for half in range(2):
                        heads = slice(half * HH, (half + 1) * HH)
                        dve.wait_ge(s_max, 2 * t + half + 1)
                        src = sm[:, u % 2, heads, :] if half else SA[:, :].rearrange("p (h k) -> p h k", k=L)
                        nc.vector.tensor_tensor(sm[:, u % 2, heads, :], src,
                                                smax[:, heads].unsqueeze(2).broadcast_to([P, HH, L]),
                                                ALU.subtract).then_inc(s_sub, 1)

                def normalise(t):
                    dve.wait_ge(s_tq, t + 1)
                    y = YB[:, :].rearrange("r (j m) -> r j m", m=VM)
                    nc.vector.reciprocal(rden[:, :, :], y[:, :, 4 * DH:4 * DH + 2]).then_inc(s_rden, 1)
                    dve.wait_ge(s_rden, t + 1)
                    for b in range(2):
                        r = slice(b * 64, b * 64 + 64)
                        last = nc.vector.tensor_tensor(
                            on[r, :].rearrange("r (j p c) -> r j p c", p=2, c=DH),
                            y[r, :, 2 * DH * b:2 * DH * (b + 1)].rearrange("r j (p c) -> r j p c", p=2),
                            rden[r, :, :].unsqueeze(3).broadcast_to([64, J, 2, DH]), ALU.mult)
                    last.then_inc(s_norm, 1)

                def residual(t, u, par, stored):
                    dve.wait_ge(s_y, t + 1)
                    dve.wait_ge(s_xres, t + 1)
                    if stored is not None:
                        dve.wait_ge(s_x1st[par][u], stored)
                    nc.vector.tensor_tensor(x1[:, par, u, :], YB[:, P:2 * P], x_res[:, u, :], ALU.add).then_inc(s_res, 1)

                def ln2_stats(r, par):
                    dve.wait_ge(s_res, 4 * r + 4)
                    for u in range(U):
                        last = nc.vector.bn_stats(stat2[:, u, :], x1[:, par, u, :])
                    last.then_inc(s_st2, 1)

                def ln2_variance():
                    for u in range(U):
                        last = nc.vector.bn_aggr(mv2[:, u, :], stat2[:, u, :])
                    last.then_inc(s_mv2, 1)

                def wide(v):
                    return v[:, :].unsqueeze(2).broadcast_to([P, U, E])

                def take_logits(r):
                    dve.wait_ge(s_rl, r + 1)
                    if runs(r, 1):
                        dve.wait_ge(s_rex, r)
                    nc.vector.tensor_copy(lg[:, :, :], YB[:, LOGITS:LOGITS + U * E].rearrange("p (u e) -> p u e", e=E)
                                          ).then_inc(s_lg, 1)
                    dve.wait_ge(s_lg, r + 1)
                    nc.vector.reduce_max(r_max[:, :], lg[:, :, :], AX).then_inc(s_ch, 1)
                    dve.wait_ge(s_ch, r * CH + 1)
                    nc.vector.tensor_tensor(lg[:, :, :], lg[:, :, :], wide(r_max), ALU.subtract).then_inc(s_lsh, 1)

                def gate_probs(r):
                    def link(n, ins):
                        ins.then_inc(s_ch, 1)
                        dve.wait_ge(s_ch, r * CH + n)

                    dve.wait_ge(s_rex, r + 1)
                    link(2, nc.vector.reduce_sum(r_sum[:, :], ex[:, :, :], AX))
                    link(3, nc.vector.reciprocal(r_inv[:, :], r_sum[:, :]))
                    link(4, nc.vector.tensor_tensor(probs[:, :, :], ex[:, :, :], wide(r_inv), ALU.mult))

                def find_two_largest(r):
                    for u in range(U):
                        nc.vector.max(largest[:, u, :], probs[:, u, :]).then_inc(s_ch, 1)
                    dve.wait_ge(s_ch, r * CH + 8)
                    nc.vector.tensor_copy(two_largest[:, :, 0:KTOP], largest[:, :, 0:KTOP]).then_inc(s_ch, 1)

                def select(r):
                    for u in range(U):
                        last = nc.vector.match_replace(left[:, u, :], two_largest[:, u, :], probs[:, u, :], -1.0)
                    last.then_inc(s_left, 1)
                    dve.wait_ge(s_left, r + 1)
                    nc.vector.tensor_tensor(sel16[:, :, :], left[:, :, :], probs[:, :, :], ALU.not_equal
                                            ).then_inc(s_sel, 1)
                    dve.wait_ge(s_sel, r + 1)

                def write_gates(r, ir, par):
                    if runs(r, 2) and par < 2:
                        dve.wait_ge(s_scat[par], 16 * KTOP * U * ir)
                    nc.vector.tensor_tensor(rows[:, par, :, RGATE:RGATE + E], sel16[:, :, :], probs[:, :, :], ALU.mult
                                            ).then_inc(s_gate, 1)

                def count_tokens(r):
                    dve.wait_ge(s_rank, r + 1)
                    nc.vector.tensor_tensor(rank[:, :, :], YB[:, RANKS:COUNTS].rearrange("p (u e) -> p u e", e=E),
                                            run_s[:, :].unsqueeze(1).broadcast_to([P, U, E]), ALU.add
                                            ).then_inc(s_pch, 1)
                    dve.wait_ge(s_pch, PCH * r + 1)
                    nc.vector.tensor_tensor(run_s[:, :], YB[:, COUNTS:COUNTS + E], run_s[:, :], ALU.add
                                            ).then_inc(s_pch, 1)

                def positions(r, par):
                    dve.wait_ge(s_pch, PCH * r + 2)
                    nc.vector.tensor_tensor(rank[:, :, :], rank[:, :, :], sel16[:, :, :], ALU.mult).then_inc(s_pch, 1)
                    dve.wait_ge(s_pch, PCH * r + 3)
                    nc.vector.reduce_max(pos_f[:, 0, :], rank[:, :, :], AX).then_inc(s_pch, 1)
                    nc.vector.reduce_sum(pos_f[:, 1, :], rank[:, :, :], AX).then_inc(s_pch, 1)
                    dve.wait_ge(s_pch, PCH * r + 5)
                    nc.vector.tensor_copy(pos[:, par, 0, :], pos_f[:, 0, :]).then_inc(s_pch, 1)
                    nc.vector.tensor_tensor(pos[:, par, 1, :], pos_f[:, 1, :], pos_f[:, 0, :], ALU.subtract
                                            ).then_inc(s_pos, 1)

                nc.vector.memset(q2[:, :, :, :, :], 0.0).then_inc(s_zero, 1)
                nc.vector.memset(ones16[:, :], 1.0).then_inc(s_zero, 1)
                nc.vector.memset(rows[:, :, :, :], 0.0).then_inc(s_zero, 1)
                nc.vector.memset(two_largest[:, :, :], -2.0).then_inc(s_two, 1)
                ln1_stats(0)
                dve.wait_ge(s_st1, 1)
                ln1_variance()
                dve.wait_ge(s_w, 16 * NW)
                nc.vector.tensor_scalar(bq_scaled[:, :], bq_s[:, :], SCALE, None, ALU.mult).then_inc(s_bqs, 1)
                x_evac(0)
                dve.wait_ge(s_w2, 16 * NW2)
                make_mask(0, 0)
                ln1_stats(1)
                dve.wait_ge(s_st1, 2)
                dve.wait_ge(s_r1, 1)
                ln1_variance()
                nc.vector.tensor_copy(bvb_s[:, :], bv_s[:, 0:1].broadcast_to([P, P])).then_inc(s_bvb, 1)
                for u in range(U):
                    last = nc.vector.tensor_copy(vx[:, u, :, :], ones_s[:, :].unsqueeze(1).broadcast_to([P, J, VM]))
                last.then_inc(s_zero, 1)
                dve.wait_ge(s_two, 1)
                dve.wait_ge(s_neg, 1)
                row_maxima(0, 0, 0)
                subtract_maxima(0, 0)
                dve.wait_ge(s_cv_ps, 1)
                nc.vector.tensor_tensor(cvec[:, :], YB[:, 0:D], bo_s[:, :], ALU.add).then_inc(s_cvec, 1)
                dve.wait_ge(s_w3, 16 * NW3)

                def body(s, i, par):
                    for u in range(U):
                        t = s * U + u
                        before = u or runs(s, 1)
                        after = u < U - 1 or runs(s, 0, NS - 2)
                        ahead = runs(s, 0, NS - 3)
                        if after:
                            if u or runs(s, 1):
                                dve.wait_ge(s_pt, 2 * t)
                            if u == 3:
                                dve.wait_ge(s_neg, s + 2)
                            row_maxima(t + 1, (u + 1) % U, par if u < 3 else 1 - par)
                        if u > 1 or runs(s, 1):
                            ppar, pi = (par, i) if u > 1 else (1 - par, i - 1 + par)
                            if u == 2 and runs(s, 2):
                                dve.wait_ge(s_xn2, s - 1)
                            residual(t - 2, (u - 2) % U, ppar, 16 * pi if runs(s, 2 if u > 1 else 3) else None)
                        if u == 0 and runs(s, 3):
                            count_tokens(s - 3)
                        if u == 2 and runs(s, 2):
                            take_logits(s - 2)
                        if after:
                            if u == 1 and ahead:
                                dve.wait_ge(s_st1, s + 3)
                                dve.wait_ge(s_r1, s + 2)
                            if u == 2 and runs(s, 1):
                                dve.wait_ge(s_st2, s)
                                if runs(s, 2):
                                    dve.wait_ge(s_r2, s - 1)
                            if u == 3 and runs(s, 2):
                                dve.wait_ge(s_ch, (s - 2) * CH + 4)
                            subtract_maxima(t + 1, (u + 1) % U)
                        elif u == 3:
                            dve.wait_ge(s_ch, (s - 2) * CH + 4)
                        if u == 0 and runs(s, 3):
                            positions(s - 3, 1 - par)
                        if u == 1 and ahead:
                            ln1_variance()
                        if u == 2 and runs(s, 1):
                            ln2_variance()
                        if u == 3 and runs(s, 2):
                            find_two_largest(s - 2)
                        if before:
                            if u == 3 and runs(s, 2):
                                dve.wait_ge(s_ch, (s - 2) * CH + 9)
                            normalise(t - 1)
                        if u == 0 and runs(s, 0, NS - 2):
                            x_evac(s + 1)
                            make_mask(s + 1, 1 - par)
                        if u == 0 and ahead:
                            ln1_stats(s + 2)
                        if u == 1 and runs(s, 1):
                            ln2_stats(s - 1, 1 - par)
                        if u == 2 and runs(s, 2):
                            gate_probs(s - 2)
                        if u == 3 and runs(s, 2):
                            select(s - 2)
                            write_gates(s - 2, i - 1, par)

                for s in range(4):
                    body(s, s // 2, s % 2)
                with dve.Fori(2, NS // 2 - 2) as i:
                    for par in range(2):
                        body(2 * i + par, i, par)
                for s in range(NS - 4, NS):
                    body(s, s // 2, s % 2)
                residual(NT - 2, U - 2, 1, 16 * (NS // 2 - 1))
                count_tokens(NS - 3)
                positions(NS - 3, 1)
                nc.vector.tensor_tensor(early_count[:, :], run_s[:, :], region_s[:, :], ALU.subtract).then_inc(s_early, 1)
                dve.wait_ge(s_early, 1)
                normalise(NT - 1)
                residual(NT - 1, U - 1, 1, 16 * (NS // 2 - 1))
                ln2_stats(NS - 1, 1)
                dve.wait_ge(s_st2, NS)
                dve.wait_ge(s_r2, NS - 1)
                ln2_variance()
                take_logits(NS - 2)
                gate_probs(NS - 2)
                find_two_largest(NS - 2)
                dve.wait_ge(s_ch, (NS - 2) * CH + 9)
                select(NS - 2)
                write_gates(NS - 2, NS // 2 - 1, 0)
                count_tokens(NS - 2)
                positions(NS - 2, 0)
                take_logits(NS - 1)
                gate_probs(NS - 1)
                find_two_largest(NS - 1)
                dve.wait_ge(s_ch, (NS - 1) * CH + 9)
                select(NS - 1)
                write_gates(NS - 1, NS // 2 - 1, 2)
                count_tokens(NS - 1)
                positions(NS - 1, 2)

                k = [0]

                def link(ins):
                    k[0] += 1
                    ins.then_inc(s_tab, 1)
                    dve.wait_ge(s_tab, k[0])

                def over_blocks(v, n=NB):
                    return v[:, :].unsqueeze(1).broadcast_to([P, n, E])

                def over_experts(v, n=NB):
                    return v[:, 0:n].unsqueeze(2).broadcast_to([P, n, E])

                nc.vector.tensor_copy(tails[:, :], run_s[:, :]).then_inc(s_tails, 1)
                link(nc.vector.tensor_tensor(count[:, :], run_s[:, :], region_s[:, :], ALU.subtract))
                link(nc.vector.tensor_tensor(skipped[:, :, :], block_rows[:, :, :], over_blocks(count), ALU.is_lt))
                link(nc.vector.reduce_sum(blocks_of[:, :], skipped[:, :, :].rearrange("p b e -> p e b"), AX))
                link(nc.vector.tensor_tensor(up_to[:, :, :], up_to[:, :, :], over_blocks(blocks_of, E), ALU.mult))
                link(nc.vector.reduce_sum(ends[:, :], up_to[:, :, :], AX))
                link(nc.vector.tensor_tensor(past[:, :, :], over_blocks(ends), blocks_s[:, :, :], ALU.is_le))
                nc.vector.reduce_sum(of_block[:, :], past[:, :, :], AX).then_inc(s_ofb, 1)
                link(nc.vector.tensor_tensor(skipped[:, :, :], past[:, :, :], over_blocks(blocks_of), ALU.mult))
                link(nc.vector.reduce_sum(start_of[:, :], skipped[:, :, :], AX))
                link(nc.vector.tensor_tensor(start_of[:, :], blocks_s[:, :, 0], start_of[:, :], ALU.subtract))
                dve.wait_ge(s_ofb, 1)
                link(nc.vector.tensor_scalar(active[:, :], of_block[:, :], float(E), None, ALU.is_lt))
                link(nc.vector.tensor_scalar(row_f[:, :], of_block[:, :], float(REG), None, ALU.mult))
                link(nc.vector.scalar_tensor_tensor(out=row_f[:, :], in0=start_of[:, :], scalar=float(BLK),
                                                    in1=row_f[:, :], op0=ALU.mult, op1=ALU.add))
                link(nc.vector.scalar_tensor_tensor(out=row_f[:, :], in0=row_f[:, :], scalar=count[:, 0:1],
                                                    in1=active[:, :], op0=ALU.subtract, op1=ALU.mult))
                nc.vector.tensor_tensor(table[:, 1, :], of_block[:, :], active[:, :], ALU.mult).then_inc(s_tabd, 1)
                link(nc.vector.tensor_tensor(table[:, 0, :], row_f[:, :], count[:, 0:1].broadcast_to([P, NB]), ALU.add))
                assert k[0] == TABLE_LINKS
                link(nc.vector.tensor_tensor(first_oh[:, :, :], over_blocks(experts_s, R3), over_experts(of_block, R3),
                                             ALU.is_equal))
                link(nc.vector.tensor_tensor(first_oh[:, :, :], first_oh[:, :, :], over_blocks(early_count, R3), ALU.mult))
                link(nc.vector.reduce_sum(had[:, :], first_oh[:, :, :], AX))
                link(nc.vector.tensor_scalar(had[:, :], had[:, :], float(-BLK), 1.0 / BLK, ALU.add, ALU.mult))
                link(nc.vector.tensor_tensor(had[:, :], start_of[:, 0:R3], had[:, :], ALU.is_le))
                link(nc.vector.tensor_scalar(sent[:, 1, :], had[:, :], float(-16 * E), float(16 + 16 * E),
                                             ALU.mult, ALU.add))
                nc.vector.tensor_scalar(sent[:, 0, :], had[:, :], float(-16 * KTOP * U), float(16 * KTOP * U * (NS // 2)),
                                        ALU.mult, ALU.add).then_inc(s_tabd, 1)
                link(nc.vector.memset(same[:, :], 0.0))
                link(nc.vector.tensor_tensor(same[:, 1:NB], of_block[:, 1:NB], of_block[:, 0:NB - 1], ALU.is_equal))
                link(nc.vector.tensor_tensor(same[:, :], same[:, :], active[:, :], ALU.mult))
                link(nc.vector.tensor_tensor(same[:, :], rounds_s[:, :], same[:, :], ALU.subtract))
                nc.vector.tensor_scalar(table[:, 2, :], same[:, :], float(16 * BT), None, ALU.mult).then_inc(s_tabw, 1)
                link(nc.vector.tensor_tensor(of_block[:, :], of_block[:, :], active[:, :], ALU.mult))
                link(nc.vector.tensor_tensor(expert_oh[:, :, :], over_blocks(experts_s), over_experts(of_block),
                                             ALU.is_equal))

                def pick_gates(b, i, r):
                    dve.wait_ge(s_xb[r], 16 * i + 16)
                    if not (isinstance(b, int) and b < R3):
                        dve.wait_ge(s_yb, b)
                    nc.vector.tensor_tensor(gtmp[:, :, :], xb[:, r, :, RGATE:RGATE + E],
                                            expert_oh[:, bass.ds(b, 1), :].broadcast_to([P, BT, E]), ALU.mult
                                            ).then_inc(s_gm, 1)
                    dve.wait_ge(s_gm, b + 1)
                    nc.vector.reduce_sum(gate[:, r, :], gtmp[:, :, :], AX).then_inc(s_gt, 1)

                def gated(b, i, r):
                    dve.wait_ge(s_gt, b + 1)
                    if not (isinstance(b, int) and b < R3):
                        dve.wait_ge(s_add[r], 16 * BT * i)
                    dve.wait_ge(s_dn, b + 1)
                    nc.vector.tensor_tensor(yb[:, r, :, :],
                                            DBK[r][:, 0:BT * D].rearrange("p (u d) -> p u d", d=D),
                                            gate[:, r, :].unsqueeze(2).broadcast_to([P, BT, D]), ALU.mult
                                            ).then_inc(s_yb, 1)

                for b in range(R3):
                    pick_gates(b, 0, b)
                    gated(b, 0, b)
                with dve.Fori(1, NB // R3) as i:
                    for r in range(R3):
                        pick_gates(R3 * i + r, i, r)
                        gated(R3 * i + r, i, r)

            @block.gpsimd
            def _(pool):
                def add_positions(s):
                    pool.wait_ge(s_ck, 16 * (s + 1))
                    v = ctx_k[:, :].rearrange("p (b k) -> p b k", k=L)
                    nc.gpsimd.tensor_tensor(v, v, pe_s[:, :].unsqueeze(1).broadcast_to([P, 2 * U, L]),
                                            ALU.add).then_inc(s_cp, 1)

                def rstd_1(s):
                    pool.wait_ge(s_stat, s + 1)
                    if runs(s, 1):
                        pool.wait_ge(s_xn, s)
                    nc.gpsimd.tensor_tensor(var1[:, :], mv1[:, :, 1], eps_s[:, :], ALU.add).then_inc(s_va1, 1)
                    nc.gpsimd.tensor_tensor(shift1[:, :], mv1[:, :, 0], minus_one[:, :], ALU.mult).then_inc(s_va1, 1)
                    pool.wait_ge(s_va1, 3 * s + 2)
                    nc.gpsimd.tensor_tensor(rstd1[:, :], var1[:, :], minus_half[:, :], ALU.pow).then_inc(s_va1, 1)
                    pool.wait_ge(s_va1, 3 * s + 3)
                    nc.gpsimd.tensor_tensor(shift1[:, :], shift1[:, :], rstd1[:, :], ALU.mult).then_inc(s_r1, 1)

                def spread_keys(t, u, par, reused=True):
                    if reused:
                        pool.wait_ge(s_sc, 2 * (t - 4) + 2)
                    for half in range(2):
                        last = nc.gpsimd.tensor_tensor(
                            kx[:, u, half, :, :], k2[:, par, half, u, :].unsqueeze(1).broadcast_to([P, HH, L]),
                            headmask[:, :].unsqueeze(2).broadcast_to([P, HH, L]), ALU.mult)
                    last.then_inc(s_kx, 1)

                def residual_bias(s, u):
                    pool.wait_ge(s_xr[u], 16 * (s + 1))
                    nc.gpsimd.tensor_tensor(x_res[:, u, :], x_res[:, u, :], cvec[:, :], ALU.add).then_inc(s_xres, 1)

                nc.gpsimd.memset(minus_half[:, :], -0.5).then_inc(s_mh, 1)
                nc.gpsimd.memset(eps_s[:, :], EPS).then_inc(s_mh, 1)
                nc.gpsimd.memset(minus_one[:, :], -1.0).then_inc(s_mh, 1)
                nc.gpsimd.memset(step_u[:, :], U * P).then_inc(s_mh, 1)
                nc.gpsimd.memset(zero_u[:, :], 0).then_inc(s_mh, 1)
                pool.wait_ge(s_mh, 5)
                pool.wait_ge(s_w, 16 * NW)
                add_positions(0)
                rstd_1(0)
                pool.wait_ge(s_w2, 16 * NW2)
                pool.wait_ge(s_kev, 1)
                spread_keys(0, 0, 0, False)
                add_positions(1)
                rstd_1(1)
                spread_keys(1, 1, 0, False)
                spread_keys(2, 2, 0, False)
                add_positions(2)
                pool.wait_ge(s_cvec, 1)
                pool.wait_ge(s_w3, 16 * NW3)

                def rstd_2(r):
                    pool.wait_ge(s_mv2, r + 1)
                    if runs(r, 1):
                        pool.wait_ge(s_xn2, r)
                    nc.gpsimd.tensor_tensor(var2[:, :], mv2[:, :, 1], eps_s[:, :], ALU.add).then_inc(s_va2, 1)
                    nc.gpsimd.tensor_tensor(shift2[:, :], mv2[:, :, 0], minus_one[:, :], ALU.mult).then_inc(s_va2, 1)
                    pool.wait_ge(s_va2, 3 * r + 2)
                    nc.gpsimd.tensor_tensor(rstd2[:, :], var2[:, :], minus_half[:, :], ALU.pow).then_inc(s_va2, 1)
                    pool.wait_ge(s_va2, 3 * r + 3)
                    nc.gpsimd.tensor_tensor(shift2[:, :], shift2[:, :], rstd2[:, :], ALU.mult).then_inc(s_r2, 1)

                def number_rows(r, par):
                    if runs(r, 1):
                        pool.wait_ge(s_tokadd, r)
                    pool.wait_ge(s_gate, r + 1)
                    pool.wait_ge(s_xn2, r + 1)
                    pool.wait_ge(s_pos, r + 1)
                    nc.gpsimd.tensor_tensor(rows[:, par, :, RTOK].bitcast(U32), tok_s[:, :], zero_u[:, :], ALU.add
                                            ).then_inc(s_tok, 1)
                    pool.wait_ge(s_tok, r + 1)
                    nc.gpsimd.tensor_tensor(tok_s[:, :], tok_s[:, :], step_u[:, :], ALU.add).then_inc(s_tokadd, 1)

                def scatter_rows(buf, tiles):
                    for u in tiles:
                        for k in range(KTOP):
                            nc.gpsimd.indirect_dma_start(
                                out=rows_d, out_offset=bass.IndirectOffsetOnAxis(ap=pos[:, buf, k, u:u + 1], axis=0),
                                in_=rows[:, buf, u, :], in_offset=None).then_inc(s_scat[min(buf, 1)], 16)

                def body(s, par):
                    for u in range(U):
                        residual_bias(s, u)
                        if u == 0:
                            spread_keys(4 * s + 3, 3, par, runs(s, 1))
                            if runs(s, 3):
                                number_rows(s - 3, 1 - par)
                                scatter_rows(1 - par, (0, 1))
                        elif runs(s, 0, NS - 2):
                            if u == 1:
                                pool.wait_ge(s_kev, s + 2)
                            spread_keys(4 * s + 3 + u, u - 1, 1 - par)
                        if u == 1:
                            if runs(s, 0, NS - 3):
                                rstd_1(s + 2)
                            if runs(s, 3):
                                scatter_rows(1 - par, (2,))
                        if u == 2:
                            if runs(s, 1):
                                rstd_2(s - 1)
                            if runs(s, 3):
                                scatter_rows(1 - par, (3,))
                        if u == 3 and runs(s, 0, NS - 4):
                            add_positions(s + 3)

                for s in range(4):
                    body(s, s % 2)
                with pool.Fori(2, NS // 2 - 2) as i:
                    for par in range(2):
                        body(2 * i + par, par)
                for s in range(NS - 4, NS):
                    body(s, s % 2)
                number_rows(NS - 3, 1)
                scatter_rows(1, range(U - 1))
                rstd_2(NS - 1)
                scatter_rows(1, (U - 1,))
                number_rows(NS - 2, 0)
                scatter_rows(0, range(U))
                pool.wait_ge(s_scat[1], 16 * KTOP * U * (NS // 2 - 1))
                number_rows(NS - 1, 2)
                scatter_rows(2, range(U))
                for par in range(2):
                    pool.wait_ge(s_scat[par], 16 * KTOP * U * (NS // 2))

                def tokens_of(r, loads):
                    pool.wait_ge(s_xb[r], 16 * loads)
                    nc.gpsimd.tensor_tensor(token[:, r, :], xb[:, r, :, RTOK].bitcast(U32), zero_u[:, 0:BT], ALU.add
                                            ).then_inc(s_tk, 1)

                def add_block(b, i, r):
                    if isinstance(b, int) and (b <= R3 or b == NB - 1):
                        if b:
                            pool.wait_ge(s_add[(r - 1) % R3], 16 * BT * ((b - 1) // R3 + 1))
                    else:
                        pool.wait_ge(s_add[(r - 2) % R3], 16 * BT * (i + 1 if r == 2 else i))
                        needed = nc.values_load(table[0:1, 2, bass.ds(b, 1)], engines=[mybir.EngineType.Pool],
                                                min_val=16 * BT, max_val=16 * BT * (NB // R3))
                        pool.wait_ge(s_add[(r - 1) % R3], needed)
                    pool.wait_ge(s_yb, b + 1)
                    pool.wait_ge(s_tk, b + 1)
                    if not (isinstance(b, int) and b == NB - 1):
                        tokens_of((r + 1) % R3, i + 1 + (r + 1) // R3)
                    for u in range(BT):
                        nc.gpsimd.indirect_dma_start(
                            out=out, out_offset=bass.IndirectOffsetOnAxis(ap=token[:, r, u:u + 1], axis=0),
                            in_=yb[:, r, u, :], in_offset=None, compute_op=ALU.add).then_inc(s_add[r], 16)

                pool.wait_ge(s_tabw, 1)
                pool.wait_ge(s_init, 16)
                for par in range(2):
                    for u in range(U):
                        pool.wait_ge(s_x1st[par][u], 16 * (NS // 2))
                tokens_of(0, 1)
                for b in range(2 * R3):
                    add_block(b, b // R3, b % R3)
                with pool.Fori(2, NB // R3 - 1) as i:
                    for r in range(R3):
                        add_block(R3 * i + r, i, r)
                for r in range(R3):
                    add_block(NB - R3 + r, NB // R3 - 1, r)
                for r in range(R3):
                    pool.wait_ge(s_add[r], 16 * BT * (NB // R3))


def kernel(x, ctx_1024, mask_BxS2_bk0, L0_xattn_Wq, L0_xattn_bq, L0_xattn_Wk, L0_xattn_bk, L0_xattn_Wv, L0_xattn_bv,
           L0_xattn_Wo, L0_xattn_bo, L0_ffn_wg1, L0_ffn_bg1, L0_ffn_wg2, L0_ffn_w_in, L0_ffn_w_out):
    import concourse.bacc as bacc
    from concourse.bass_utils import run_bass_kernel_spmd

    def laid(a, *shape):
        a = np.asarray(a)
        return np.ascontiguousarray(a.reshape(shape) if shape else a)

    def turned(a):
        return np.ascontiguousarray(np.asarray(a).T)

    arrays = {
        "x": laid(x, N, D),
        "ctx_t": turned(laid(ctx_1024, N, D)),
        "mask": laid(mask_BxS2_bk0),
        "wq_t": turned(L0_xattn_Wq), "bq": laid(L0_xattn_bq),
        "wk_t": turned(L0_xattn_Wk), "bk": laid(L0_xattn_bk),
        "wv_t": turned(L0_xattn_Wv), "bv": laid(L0_xattn_bv),
        "wo_t": turned(L0_xattn_Wo), "bo": laid(L0_xattn_bo),
        "wg1": laid(L0_ffn_wg1), "bg1": laid(L0_ffn_bg1), "wg2": laid(L0_ffn_wg2),
        "w_in": laid(L0_ffn_w_in), "w_out": laid(L0_ffn_w_out),
    }
    nc = bacc.Bacc("TRN2", target_bir_lowering=False, num_devices=1)
    ins = [nc.dram_tensor(n, a.shape, mybir.dt.from_np(a.dtype), kind="ExternalInput").ap() for n, a in arrays.items()]
    out = nc.dram_tensor("out", [N + BLK, D], F32, kind="ExternalOutput").ap()
    build(nc, *ins, out)
    r = run_bass_kernel_spmd(nc, [arrays], core_ids=[0])
    return r.results[0]["out"][:N].reshape(B, L, D)
```
